# Optimizing a Trainium2 kernel written in Bass

```python
import numpy as np
import jax
import jax.numpy as jnp

def _softmax(x, axis=-1):
    return jax.nn.softmax(x, axis=axis)

def _gelu(x):
    return jax.nn.gelu(x, approximate=True)

def _silu(x):
    return jax.nn.silu(x)

def _sigmoid(x):
    return jax.nn.sigmoid(x)

def _layernorm(x, axis=-1, eps=1e-05):
    m = jnp.mean(x, axis=axis, keepdims=True)
    v = jnp.var(x, axis=axis, keepdims=True)
    return (x - m) / jnp.sqrt(v + eps)

def _scatter_add(tgt, idx, src, axis=0):
    return tgt.at[idx].add(src)

def _segment_sum(src, seg, n):
    return jax.ops.segment_sum(src, seg, n)
kernel_name = 'mk_adj_resnorm_d4_adj_r2_1a0648'

def setup_inputs(seed: int=0):
    np.random.seed(seed)
    _w = jnp.asarray

    def _rec_inputs():
        import jax
        import jax.numpy as jnp
        _gk = jax.random.key(seed)
        x = -0.000929 + 1 * jax.random.normal(jax.random.fold_in(_gk, 1), (3327, 64), jnp.float32)
        _a = jax.random.bernoulli(jax.random.fold_in(_gk, 2), 0.00240457, (3327, 3327))
        _a = jnp.logical_or(_a, jnp.swapaxes(_a, -1, -2))
        _a = jnp.logical_or(_a, jnp.eye(3327, dtype=bool))
        _af = _a.astype(jnp.float32)
        _af = _af * jax.random.uniform(jax.random.fold_in(_gk, 3), (3327, 3327), jnp.float32, 0.05, 0.0423436)
        adj = _af
        return (x, adj)
    x, adj = _rec_inputs()

    def _L0_gnn_setup():
        import jax, jax.numpy as jnp
        import numpy as np
        N, F_IN, F_OUT, K = (8192, 64, 64, 3)
        key = jax.random.key(seed)
        k1, k2, k3, k4 = jax.random.split(key, 4)
        x = jax.random.normal(k1, (N, F_IN), dtype=jnp.float32)
        L_tilde = jax.random.normal(k2, (N, N), dtype=jnp.float32) / np.float32(np.sqrt(N))
        stdv = 1.0 / np.sqrt(F_OUT)
        weights = jax.random.uniform(k3, (K + 1, F_IN, F_OUT), dtype=jnp.float32, minval=-stdv, maxval=stdv)
        bias = jax.random.uniform(k4, (F_OUT,), dtype=jnp.float32, minval=-stdv, maxval=stdv)
        return {'x': x, 'L_tilde': L_tilde, 'weights': weights, 'bias': bias}
    _L0_gnn_all = _L0_gnn_setup()
    _L0_gnn_in = {k: v for k, v in _L0_gnn_all.items() if k in ('weights', 'bias')}
    del _L0_gnn_all

    def _L1_gnn_setup():
        import jax, jax.numpy as jnp
        import numpy as np
        N, D, H = (8192, 64, 128)
        GAIN = 0.2
        key = jax.random.key(seed)
        ks = jax.random.split(key, 6)
        X = jax.random.normal(ks[0], (N, D), dtype=jnp.float32)
        t = jax.random.uniform(ks[1], (1,), dtype=jnp.float32)
        Wt = jax.random.uniform(ks[2], (N, N), dtype=jnp.float32)
        B = GAIN * jnp.eye(D, dtype=jnp.float32) + 0.01 * jax.random.normal(ks[3], (D, D), dtype=jnp.float32)
        W1 = jax.random.normal(ks[4], (D + 1, H), dtype=jnp.float32) * (1.0 / np.sqrt(D + 1))
        b1 = jnp.zeros((H,), dtype=jnp.float32)
        W2 = jax.random.normal(ks[5], (H, D), dtype=jnp.float32) * (1.0 / np.sqrt(H))
        b2 = jnp.zeros((D,), dtype=jnp.float32)
        return {'X': X, 't': t, 'Wt': Wt, 'B': B, 'W1': W1, 'b1': b1, 'W2': W2, 'b2': b2}
    _L1_gnn_all = _L1_gnn_setup()
    _L1_gnn_in = {k: v for k, v in _L1_gnn_all.items() if k in ('t', 'B', 'W1', 'b1', 'W2', 'b2')}
    del _L1_gnn_all

    def _L2_gnn_setup():
        import jax, jax.numpy as jnp
        import numpy as np
        N, D_IN, D_OUT = (4096, 64, 64)
        MAX_NEIGH = 100
        DECAY = 0.5
        key = jax.random.key(seed)
        k1, k2, k3, k4 = jax.random.split(key, 4)
        stdv = 1.0 / np.sqrt(D_OUT)
        inputs = {'input': jax.random.normal(k1, (N, D_IN), dtype=jnp.float32), 'adj': jax.random.randint(k2, (N, N), 0, 2).astype(jnp.float32), 'weight': jax.random.uniform(k3, (D_IN, D_OUT), minval=-stdv, maxval=stdv, dtype=jnp.float32), 'bias': jax.random.uniform(k4, (D_OUT,), minval=-stdv, maxval=stdv, dtype=jnp.float32)}
        return inputs
    _L2_gnn_all = _L2_gnn_setup()
    _L2_gnn_in = {k: v for k, v in _L2_gnn_all.items() if k in ('weight', 'bias')}
    del _L2_gnn_all

    def _L3_gnn_setup():
        import jax, jax.numpy as jnp
        import numpy as np
        CURV = 1.0
        MIN_NORM = 1e-15
        TANH_CLIP = 1.0 - 1e-05

        def _mobius_add(x, y, c):
            x2 = jnp.sum(x * x, axis=-1, keepdims=True)
            y2 = jnp.sum(y * y, axis=-1, keepdims=True)
            xy = jnp.sum(x * y, axis=-1, keepdims=True)
            num = (1.0 + 2.0 * c * xy + c * y2) * x + (1.0 - c * x2) * y
            den = 1.0 + 2.0 * c * xy + c ** 2 * x2 * y2
            return num / jnp.maximum(den, MIN_NORM)

        def _logmap(x, y, c):
            sub = _mobius_add(-x, y, c)
            sub_norm = jnp.maximum(jnp.linalg.norm(sub, axis=-1, keepdims=True), MIN_NORM)
            x2 = jnp.sum(x * x, axis=-1, keepdims=True)
            lam_x = 2.0 / jnp.maximum(1.0 - c * x2, MIN_NORM)
            sqrt_c = jnp.sqrt(c)
            arg = jnp.clip(sqrt_c * sub_norm, 0.0, TANH_CLIP)
            return 2.0 / (sqrt_c * lam_x) * jnp.arctanh(arg) * sub / sub_norm

        def _expmap(x, v, c):
            v_norm = jnp.maximum(jnp.linalg.norm(v, axis=-1, keepdims=True), MIN_NORM)
            x2 = jnp.sum(x * x, axis=-1, keepdims=True)
            lam_x = 2.0 / jnp.maximum(1.0 - c * x2, MIN_NORM)
            sqrt_c = jnp.sqrt(c)
            second = jnp.tanh(sqrt_c * lam_x * v_norm / 2.0) * v / (sqrt_c * v_norm)
            return _mobius_add(x, second, c)
        key = jax.random.key(seed)
        k1, k2, k3 = jax.random.split(key, 3)
        N, C_IN, C_OUT = (768, 64, 64)
        x = jax.random.normal(k1, (N, C_IN), dtype=jnp.float32) * 0.03
        adj = (jax.random.uniform(k2, (N, N)) < 0.02).astype(jnp.float32)
        bound = 1.0 / np.sqrt(C_IN)
        weight = jax.random.uniform(k3, (C_IN, C_OUT), dtype=jnp.float32, minval=-bound, maxval=bound)
        bias = jnp.zeros((C_OUT,), dtype=jnp.float32)
        return {'x': x, 'adj': adj, 'weight': weight, 'bias': bias}
    _L3_gnn_all = _L3_gnn_setup()
    _L3_gnn_in = {k: v for k, v in _L3_gnn_all.items() if k in ('weight', 'bias')}
    del _L3_gnn_all
    return {'x': x, 'adj': adj, 'L0_gnn_weights': _L0_gnn_in['weights'], 'L0_gnn_bias': _L0_gnn_in['bias'], 'L1_gnn_t': _L1_gnn_in['t'], 'L1_gnn_B': _L1_gnn_in['B'], 'L1_gnn_W1': _L1_gnn_in['W1'], 'L1_gnn_b1': _L1_gnn_in['b1'], 'L1_gnn_W2': _L1_gnn_in['W2'], 'L1_gnn_b2': _L1_gnn_in['b2'], 'L2_gnn_weight': _L2_gnn_in['weight'], 'L2_gnn_bias': _L2_gnn_in['bias'], 'L3_gnn_weight': _L3_gnn_in['weight'], 'L3_gnn_bias': _L3_gnn_in['bias']}

def reference(x, adj, L0_gnn_weights, L0_gnn_bias, L1_gnn_t, L1_gnn_B, L1_gnn_W1, L1_gnn_b1, L1_gnn_W2, L1_gnn_b2, L2_gnn_weight, L2_gnn_bias, L3_gnn_weight, L3_gnn_bias):
    import jax
    import jax.numpy as jnp

    def _L0_gnn_ref(x, L_tilde, weights, bias):
        import jax, jax.numpy as jnp
        import numpy as np
        N, F_IN, F_OUT, K = (8192, 64, 64, 3)
        T_prev = x
        out = T_prev @ weights[0]
        T_curr = L_tilde @ x
        out = out + T_curr @ weights[1]
        for k in range(2, K + 1):
            T_next = 2.0 * (L_tilde @ T_curr) - T_prev
            out = out + T_next @ weights[k]
            T_prev, T_curr = (T_curr, T_next)
        return out + bias

    def _L1_gnn_ref(X, t, Wt, B, W1, b1, W2, b2):
        import jax, jax.numpy as jnp
        import numpy as np
        N, D, H = (8192, 64, 128)
        GAIN = 0.2
        n = X.shape[0]
        tcol = jnp.broadcast_to(t.reshape(1, 1), (n, 1))
        h = jnp.tanh(jnp.concatenate([X, tcol], axis=1) @ W1 + b1)
        u_intra = h @ W2 + b2
        XB = X @ B.T
        u_comm = Wt @ XB - jnp.sum(Wt, axis=1, keepdims=True) * XB
        return u_intra + u_comm

    def _L2_gnn_ref(input, adj, weight, bias):
        import jax, jax.numpy as jnp
        import numpy as np
        N, D_IN, D_OUT = (4096, 64, 64)
        MAX_NEIGH = 100
        DECAY = 0.5
        support = input @ weight
        mask = (adj != 0).astype(support.dtype)
        rank = jnp.cumsum(mask, axis=1)
        deg = rank[:, -1:]
        k = jnp.minimum(deg, float(MAX_NEIGH))
        pos = rank - (deg - k)
        w = mask * jnp.where(pos > 0, DECAY ** (k - pos), 0.0)
        out = w @ support + bias
        return out

    def _L3_gnn_ref(x, adj, weight, bias):
        import jax, jax.numpy as jnp
        import numpy as np
        CURV = 1.0
        MIN_NORM = 1e-15
        TANH_CLIP = 1.0 - 1e-05

        def _mobius_add(x, y, c):
            x2 = jnp.sum(x * x, axis=-1, keepdims=True)
            y2 = jnp.sum(y * y, axis=-1, keepdims=True)
            xy = jnp.sum(x * y, axis=-1, keepdims=True)
            num = (1.0 + 2.0 * c * xy + c * y2) * x + (1.0 - c * x2) * y
            den = 1.0 + 2.0 * c * xy + c ** 2 * x2 * y2
            return num / jnp.maximum(den, MIN_NORM)

        def _logmap(x, y, c):
            sub = _mobius_add(-x, y, c)
            sub_norm = jnp.maximum(jnp.linalg.norm(sub, axis=-1, keepdims=True), MIN_NORM)
            x2 = jnp.sum(x * x, axis=-1, keepdims=True)
            lam_x = 2.0 / jnp.maximum(1.0 - c * x2, MIN_NORM)
            sqrt_c = jnp.sqrt(c)
            arg = jnp.clip(sqrt_c * sub_norm, 0.0, TANH_CLIP)
            return 2.0 / (sqrt_c * lam_x) * jnp.arctanh(arg) * sub / sub_norm

        def _expmap(x, v, c):
            v_norm = jnp.maximum(jnp.linalg.norm(v, axis=-1, keepdims=True), MIN_NORM)
            x2 = jnp.sum(x * x, axis=-1, keepdims=True)
            lam_x = 2.0 / jnp.maximum(1.0 - c * x2, MIN_NORM)
            sqrt_c = jnp.sqrt(c)
            second = jnp.tanh(sqrt_c * lam_x * v_norm / 2.0) * v / (sqrt_c * v_norm)
            return _mobius_add(x, second, c)
        c = CURV
        deg = jnp.maximum(adj.sum(axis=1, keepdims=True), 1e-08)
        w = adj / deg
        log_ij = _logmap(x[:, None, :], x[None, :, :], c)
        agg = jnp.einsum('ij,ijc->ic', w, log_ij)
        transformed = agg @ weight + bias
        origin = jnp.zeros_like(transformed)
        return _expmap(origin, transformed, c)
    x = _layernorm(x + _L0_gnn_ref(x, adj, L0_gnn_weights, L0_gnn_bias), axis=-1)
    x = _layernorm(x + _L1_gnn_ref(x, L1_gnn_t, adj, L1_gnn_B, L1_gnn_W1, L1_gnn_b1, L1_gnn_W2, L1_gnn_b2), axis=-1)
    x = _layernorm(x + _L2_gnn_ref(x, adj, L2_gnn_weight, L2_gnn_bias), axis=-1)
    x = _layernorm(x + _L3_gnn_ref(x, adj, L3_gnn_weight, L3_gnn_bias), axis=-1)
    return x

_drawn_inputs = setup_inputs


def setup_inputs(seed=0):
    import zlib

    import numpy as np

    out = dict(_drawn_inputs(seed))
    spreads = {'L1_gnn_b1': (0.0, 0.1), 'L1_gnn_b2': (0.0, 0.1), 'L3_gnn_bias': (0.0, 0.1)}
    factors = {}
    for name, (base, spread) in spreads.items():
        noise = np.random.default_rng([zlib.crc32(name.encode()), seed]).standard_normal(out[name].shape)
        drawn = base * np.exp(spread * noise) if base else spread * noise
        out[name] = jnp.asarray(drawn.astype(out[name].dtype))
    for name, factor in factors.items():
        out[name] = (out[name] * factor).astype(out[name].dtype)
    return out
```

```python
from contextlib import ExitStack

import concourse.bass as bass
from concourse import mybir

F32 = mybir.dt.float32
BF16 = mybir.dt.bfloat16
U16 = mybir.dt.uint16
I32 = mybir.dt.int32
ALU = mybir.AluOpType
ACT = mybir.ActivationFunctionType
AX_X = mybir.AxisListType.X

P = 128
N = 3327
D = 64
NB = (N + P - 1) // P
NP = NB * P
HB = NB // 2
EPS = 1e-5

GROUPS = [3, 3, 3, 3, 3, 3, 4, 4]
START = [sum(GROUPS[:g]) for g in range(len(GROUPS))]
NG = len(GROUPS)
RING = 4
AHEAD = 2
assert sum(GROUPS) == NB and NG % RING == 0 and AHEAD < RING

CUT = 100
UNIT = 128
DIAG = 128
MASK_BIAS = float(UNIT * CUT - UNIT * DIAG)
UNSCALE = 2.0 ** 27

NEAR = 0.5
ROOT = 1.39459825
MID = -0.04442543
FAR = 1.32681359 ** 2
C3 = -0.40685946
TANH_CLIP = 1.0 - 1e-5
MIN_NORM = 1e-15
SMALL = 0.0625
SERIES = [1 / 11, 1 / 9, 1 / 7, 1 / 5, 1 / 3, 1.0]

COLS = {}
_at = 0
for _name, _w in (("ident", P), ("bt", D), ("w1", P), ("w2", D), ("bias", D), ("ones", P),
                  ("tcol", 1), ("w1t", 1), ("b1", 1), ("valid", 1)):
    COLS[_name] = (_at, _at + _w)
    _at += _w
NCONST = _at
COLS["lw2"] = (COLS["w1"][0], COLS["w1"][0] + D)
COLS["lw3"] = (COLS["w1"][0] + D, COLS["w1"][1])
BIAS_ROW = {"b2": 0, "lb2": 32, "lb3": 64}

SLOT = NB * P
SLOTS6 = 9
NF = D + 3


def gnn_kernel(nc, a_blocks, xt, wcat, consts, tri, out):
    with ExitStack() as ctx:
        def sb(name, shape, dt=F32):
            return ctx.enter_context(nc.sbuf_tensor(name, shape, dt))

        def sem(name):
            return ctx.enter_context(nc.semaphore(name))

        slots = sb("slots", [P, HB * SLOT])
        work = sb("work", [P, 8666])
        cst = sb("cst", [P, NCONST])
        tri_sb = sb("tri_sb", [P, 2, P], BF16)
        stats = sb("stats", [P, NB, 6])
        small = sb("small", [P, 8, NB])
        cols = sb("cols", [P, 12])
        hbias = cols[:, 9:10]
        flag_i = sb("flag_i", [1, 1], I32)
        banks = ctx.enter_context(nc.psum_tensor("banks", [P, 8, 512], F32))

        def const(name, rows=P):
            a, b = COLS[name]
            return cst[0:rows, a:b]

        def ones_and_bias(name):
            row = BIAS_ROW[name]
            return tuple(cst[row:row + 1, COLS[n][0]:COLS[n][1]] for n in ("ones", "bias"))

        ident = const("ident")

        a_slot = slots[:, :].rearrange("p (s j i) -> p s j i", s=HB, j=NB)
        a_flat = slots[:, :].rearrange("p (s w) -> p s w", s=HB)
        xt_sb = slots[0:D + 1, (HB - 1) * SLOT:HB * SLOT]
        M0, U0 = 0, NB * (D + 1)
        moving = work[:, M0:U0].rearrange("p (j c) -> p j c", c=D + 1)
        moving_h = work[:, M0:U0].rearrange("p (h s c) -> p h s c", h=2, c=D + 1)
        wcat_sb = work[0:D + 1, M0:M0 + 4 * D]

        def region(n):
            return work[:, U0 + n * NB * D:U0 + (n + 1) * NB * D]

        def halves(n):
            return region(n).rearrange("p (h s c) -> p h s c", h=2, c=D)

        def blocks(n):
            return region(n).rearrange("p (b c) -> p b c", c=D)

        u_all = work[:, U0:U0 + 4 * NB * D].rearrange("p (u b c) -> p u b c", u=4, c=D)
        XW3, XW2, XW1, XW0 = 0, 1, 2, 3
        X1, Y1, X2 = 0, 1, 2
        at = U0 + 3 * NB * D
        zx = work[:, at:at + 2 * P].rearrange("p (b c) -> p b c", b=2)
        zxt = work[:, at + 2 * P:at + 4 * P].rearrange("p (b c) -> p b c", b=2)
        ht = work[:, at + 4 * P:at + 6 * P].rearrange("p (b c) -> p b c", b=2)
        spl_w = NB * 3 * D // 2
        spl = work[:, 0:spl_w].bitcast(BF16).rearrange("p (j k c) -> p j k c", k=3, c=D)
        ci_w = (NB + 1) * P // 2
        ci_buf = [work[:, at:at + ci_w].bitcast(BF16), work[:, spl_w:spl_w + ci_w].bitcast(BF16)]
        wt_w = [max(GROUPS[n::RING]) * P // 2 for n in range(RING)]
        wt_at = [spl_w + ci_w + sum(wt_w[:n]) for n in range(3)] + [at + ci_w]
        wt = [work[:, a:a + w].bitcast(BF16) for a, w in zip(wt_at, wt_w)]
        aggt5 = work[0:D, wt_at[2] + wt_w[2]:wt_at[2] + wt_w[2] + P]
        assert wt_at[2] + wt_w[2] + P <= U0 + X2 * NB * D and wt_at[3] + wt_w[3] <= 8666
        tile6 = SLOTS6 * SLOT
        ut = slots[0:NF, tile6:tile6 + SLOT]
        vt = slots[0:NF, tile6 + SLOT:tile6 + 2 * SLOT]
        vt2 = slots[0:NF, tile6 + 2 * SLOT:tile6 + 3 * SLOT]
        nf_at = tile6 + 3 * SLOT
        nf = slots[:, nf_at:nf_at + NB * NF].rearrange("p (b c) -> p b c", c=NF)
        sq = [slots[:, nf_at + NB * NF + 512 * n:nf_at + NB * NF + 512 * (n + 1)] for n in range(2)]
        aggt6 = slots[0:D, nf_at + NB * NF + 1024:nf_at + NB * NF + 1024 + P]
        assert nf_at + NB * NF + 1024 + P <= HB * SLOT
        nv = work[:, 0:NB * NF].rearrange("p (b c) -> p b c", c=NF)
        v3_at = NB * NF
        v3 = work[:, v3_at:v3_at + NB * D].rearrange("p (b c) -> p b c", c=D)
        s_at = v3_at + NB * D
        st = [work[:, a:a + 512] for a in (s_at, s_at + 512, s_at + 1024, at)]
        assert s_at + 1536 <= U0 + X2 * NB * D
        x3 = blocks(X2)
        gen = [work[:, s_at + 256 * n:s_at + 256 * (n + 1)] for n in range(6)]
        gen += [work[:, at + 512 + 256 * n:at + 512 + 256 * (n + 1)] for n in range(5)]
        agg_wide = sb("agg", [P, P])
        agg = agg_wide[:, 0:D]
        neg_rs = sb("neg_rs", [P, NB])

        ld = [sem(f"slot_loaded{s}") for s in range(HB)]
        c_ld = sem("constants_loaded")
        x_ld = sem("xt_loaded")
        ld6 = sem("pass5_loaded")
        arrived = sem("blocks_arrived")
        start = sem("start")
        u_ps = sem("xw_in_psum")
        u_sb = sem("xw_in_sbuf")
        m_ready = sem("moving_ready")
        prod = sem("block_product_done")
        freed = sem("block_product_read")
        link = sem("vector_chain")
        ln_c = sem("norm_chain")
        ve = sem("variance_ready")
        rt = sem("root_ready")
        t4, c4, h4, a4, o4, y4 = (sem(f"comm_{n}") for n in ("turned", "turned_in_sbuf", "hidden", "tanh", "sum", "sum_read"))
        spl_rdy = sem("split_ready")
        ci = sem("suffix_masks_built")
        c_done = sem("counts_done")
        w_rdy = sem("weights_ready")
        w_used = sem("weights_used")
        z5, t5, c5, o5, y5 = (sem(f"decay_{n}") for n in ("sum_read", "turned", "turned_in_sbuf", "out", "out_read"))
        pm_t = sem("deviation_turned")
        pm_r = sem("flag_row")
        fl_b = sem("flag_spread")
        fl_i = sem("flag_ready")
        nat = sem("features_ready")
        ft_t = sem("features_turned")
        ft_c = sem("features_copied")
        nv2 = sem("features2_ready")
        g_done = sem("forms_done")
        q_done = sem("squares_done")
        t_rdy = sem("weights_before_a")
        sd_rdy = sem("s_ready_vector")
        sp_rdy = sem("s_ready_pool")
        s_used = sem("s_used")
        gl = sem("general_chain")
        ga = sem("general_act")
        gen_f = sem("general_last_steps")
        fin = sem("final_chain")
        gv = sem("general_to_act")
        z6, t6, c6, o6, y6 = (sem(f"ball_{n}") for n in ("agg_ready", "turned", "turned_in_sbuf", "out", "out_read"))
        a_used = sem("pass5_slot_used")
        th = sem("tanh_ready")
        vr = sem("norm_ready")
        stored = sem("stored")

        PB = 5
        LAG = 3
        W_CREDIT = NG + RING

        block = ctx.enter_context(nc.Block())

        @block.sync
        def _(sp):
            sp.dma_start(xt_sb, xt).then_inc(x_ld, 16)
            sp.dma_start(wcat_sb, wcat).then_inc(x_ld, 16)
            sp.dma_start(cst[:, :], consts).then_inc(c_ld, 16)
            sp.dma_start(tri_sb[:, :, :], tri).then_inc(c_ld, 16)
            for s in range(HB):
                if s == HB - 1:
                    sp.wait_ge(u_ps, NB)
                sp.dma_start(a_flat[:, s], a_blocks[s]).then_inc(ld[s], 16)
            with sp.Fori(1, 5) as g:
                for s in range(HB):
                    sp.wait_ge(prod, g * (2 * HB) + (s + 1 - 2 * HB))
                    sp.dma_start(a_flat[:, s], a_blocks[(g % 2) * HB + s]).then_inc(ld[s], 16)
            for s in range(HB):
                sp.wait_ge(ci, NB * (s + 1))
                sp.dma_start(a_flat[:, s], a_blocks[HB + s]).then_inc(ld[s], 16)
            with sp.Fori(SLOTS6, NB) as q:
                sp.wait_ge(a_used, q - (SLOTS6 - 1))
                sp.dma_start(a_flat[:, q % SLOTS6], a_blocks[(q + HB) % NB]).then_inc(ld6, 16)
                sp.wait_ge(ld6, 16 * q - 16 * (SLOTS6 - 1))
                sp.sem_inc(arrived, 1)
            sp.wait_ge(y6, 1 + NB + 1)
            full = N // P
            sp.dma_start(out[0:full * P].rearrange("(b p) c -> p b c", p=P), v3[:, 0:full, :]).then_inc(stored, 16)
            sp.dma_start(out[full * P:N], v3[0:N - full * P, full, :]).then_inc(stored, 16)
            sp.wait_ge(stored, 32)

        @block.gpsimd
        def _(pool):
            with pool.Fori(0, 6) as g:
                for s in range(HB):
                    pool.wait_ge(ld[s], 16 * g + 16)
                    pool.sem_inc(arrived, 1)
            pool.wait_ge(fl_i, 1)
            fast = pool.value_load(flag_i[0:1, 0:1], min_val=0, max_val=1)
            with pool.If(fast != 0):
                with pool.Fori(0, NB) as q:
                    for g in range(0, NG, 2):
                        j0, j1 = START[g], START[g] + GROUPS[g]
                        w = GROUPS[g] * P
                        pool.wait_ge(arrived, q + 5 * HB + 5)
                        pool.wait_ge(t_rdy, q * NG + (RING + g + 1))
                        s = st[g % RING][:, 0:w]
                        nc.gpsimd.tensor_tensor(s, s, a_flat[:, q % SLOTS6, j0 * P:j1 * P], ALU.mult)\
                            .then_inc(sp_rdy, 1)
            with pool.Else():
                pool.wait_ge(fl_i, 1)

        @block.tensor
        def _(pe):
            pe.wait_ge(x_ld, 32)
            pe.wait_ge(c_ld, 32)
            for b in range(NB):
                if b >= PB:
                    pe.wait_ge(u_sb, b - PB + 2)
                o = banks[:, b % PB, 0:4 * D]
                pe.matmul(o, xt_sb[:, b * P:(b + 1) * P], wcat_sb, start=True, stop=False)
                pe.matmul(o[:, 3 * D:4 * D], xt_sb[:, b * P:(b + 1) * P], const("ident", D + 1)[:, 0:D],
                          start=False, stop=True).then_inc(u_ps, 1)

            def product(n, s):
                pe.wait_ge(freed, n + 1)
                for j in range(NB):
                    last = pe.matmul(banks[:, s % PB, 0:D + 1], a_slot[:, s, j, :], moving[:, j, :],
                                     start=(j == 0), stop=(j == NB - 1))
                last.then_inc(prod, 1)

            with pe.Fori(0, 3) as p:
                with pe.Fori(0, 2) as k:
                    pe.wait_ge(m_ready, 2 * p + 2)
                    for s in range(HB):
                        pe.wait_ge(arrived, p * HB + k * HB + (s + 1))
                        product(p * (2 * HB) + k * HB + s, s)

            def turn4(n, s):
                pe.wait_ge(freed, n + (3 * NB + LAG + 1))
                pe.wait_ge(c4, n + 1)
                pe.transpose(banks[:, 5, 0:P], zx[:, s % 2, :], ident).then_inc(t4, 1)

            def hidden4(n, s):
                pe.wait_ge(c4, n + 2)
                pe.wait_ge(a4, n + 1)
                pe.matmul(banks[:, 6, 0:P], const("w1")[D:2 * D, :], zxt[D:2 * D, s % 2, :], start=True, stop=True).then_inc(h4, 1)

            def sum4(n, s):
                pe.wait_ge(a4, n + 2)
                pe.wait_ge(y4, n + 1)
                o = banks[:, 7, 0:D]
                pe.matmul(o, zxt[:, s % 2, :], const("bt"), start=True, stop=False)
                pe.matmul(o, *ones_and_bias("b2"), start=False, stop=False)
                pe.matmul(o, ht[:, s % 2, :], const("w2"), start=False, stop=True).then_inc(o4, 1)

            with pe.Fori(0, 2) as k:
                pe.wait_ge(m_ready, 8)
                for s in range(HB + 3):
                    if s < HB:
                        pe.wait_ge(arrived, k * HB + (3 * HB + s + 1))
                        product(k * HB + (6 * HB + s), s)
                    if 1 <= s <= HB:
                        turn4(k * HB + (s - 1), s - 1)
                    if 2 <= s <= HB + 1:
                        hidden4(k * HB + (s - 2), s - 2)
                    if 3 <= s:
                        sum4(k * HB + (s - 3), s - 3)

            ci_pe = [c.rearrange("p (j i) -> p j i", i=P) for c in ci_buf]

            def counts(q, g, buf):
                pe.wait_ge(ci, q * NB + NB)
                pe.wait_ge(w_rdy, q * NG + (g + 1 + NG))
                o = banks[:, 4 + g % RING, 0:GROUPS[g] * P]
                a, b = START[g], START[g] + GROUPS[g]
                pe.matmul(o, tri_sb[:, 0, :], ci_buf[buf][:, a * P:b * P], start=True, stop=False)
                pe.matmul(o, tri_sb[:, 1, :], ci_buf[buf][:, (a + 1) * P:(b + 1) * P],
                          start=False, stop=True).then_inc(c_done, 1)

            def neighbours(q, g, bank):
                pe.wait_ge(w_rdy, q * NG + (g + 1 + W_CREDIT))
                if g == 0:
                    pe.wait_ge(z5, q + 1)
                for j in range(GROUPS[g]):
                    jb = START[g] + j
                    last = pe.matmul(banks[:, bank, 0:3 * D], wt[g % RING][:, j * P:(j + 1) * P],
                                     spl[:, jb, :, :].rearrange("p k c -> p (k c)"), start=(jb == 0), stop=(jb == NB - 1))
                last.then_inc(w_used, 1)

            def turn5(q):
                pe.wait_ge(z5, q + 3)
                pe.transpose(banks[:, 2, 0:P], agg_wide[:, :], ident).then_inc(t5, 1)

            def out5(q):
                pe.wait_ge(c5, q + 1)
                pe.wait_ge(y5, q + 1)
                pe.matmul(banks[:, 3, 0:D], aggt5, const("lw2", D), start=True, stop=False)
                pe.matmul(banks[:, 3, 0:D], *ones_and_bias("lb2"), start=False, stop=True).then_inc(o5, 1)

            def steps5(q, buf, first, last):
                for g in range(NG):
                    if g + AHEAD < NG:
                        counts(q, g + AHEAD, buf)
                    elif not last:
                        counts(q + 1, g + AHEAD - NG, 1 - buf)
                    if g == 2 and not first:
                        turn5(q - 1)
                    if g == 5 and not first:
                        out5(q - 1)
                    neighbours(q, g, buf)

            for g in range(AHEAD):
                counts(0, g, 0)
            pe.wait_ge(spl_rdy, 1)
            steps5(0, 0, True, False)
            with pe.Fori(0, HB - 1) as h:
                steps5(2 * h + 1, 1, False, False)
                steps5(2 * h + 2, 0, False, False)
            steps5(NB - 1, 1, False, True)
            turn5(NB - 1)
            out5(NB - 1)

            pe.wait_ge(pm_t, 1)
            pe.transpose(banks[0:1, 2, 0:P], cols[:, 0:1], ident).then_inc(pm_r, 1)
            pe.wait_ge(pm_t, 2)
            pe.matmul(banks[:, 3, 0:1], const("ones", 1), cols[0:1, 2:3], start=True, stop=True).then_inc(fl_b, 1)
            pe.wait_ge(nat, 1)

            def turn_features(src, base):
                for b in range(NB):
                    t = base + b // 4
                    if b % 4 == 0:
                        pe.wait_ge(ft_c, t + 1)
                    last = pe.transpose(banks[0:NF, 4 + t % RING, (b % 4) * P:(b % 4 + 1) * P], src[:, b, :], ident)
                    if b % 4 == 3 or b == NB - 1:
                        last.then_inc(ft_t, 1)

            NT = (NB + 3) // 4
            turn_features(nf, 0)
            pe.wait_ge(nat, 2)
            turn_features(nv, NT)

            pe.wait_ge(fl_i, 1)
            fast = pe.value_load(flag_i[0:1, 0:1], min_val=0, max_val=1)

            def turn6(q):
                pe.wait_ge(z6, q + 3)
                pe.transpose(banks[:, 2, 0:P], agg_wide[:, :], ident).then_inc(t6, 1)

            def out6(q):
                pe.wait_ge(c6, q + 1)
                pe.wait_ge(y6, q + 1)
                pe.matmul(banks[:, 3, 0:D], aggt6, const("lw3", D), start=True, stop=False)
                pe.matmul(banks[:, 3, 0:D], *ones_and_bias("lb3"), start=False, stop=True).then_inc(o6, 1)

            def forms(q, g):
                pe.wait_ge(t_rdy, q * NG + (g + 1))
                col = (q + HB) % NB
                for j in range(GROUPS[g]):
                    jb = START[g] + j
                    last = pe.matmul(banks[:, 4 + g % RING, j * P:(j + 1) * P], ut[:, jb * P:(jb + 1) * P],
                                     vt.rearrange("p (b i) -> p b i", i=P)[:, col, :], start=True, stop=True)
                last.then_inc(g_done, 1)

            def aggregate(q, g):
                if g % 2:
                    pe.wait_ge(sd_rdy, q * (NG // 2) + (g // 2 + 1))
                else:
                    pe.wait_ge(sp_rdy, q * (NG // 2) + (g // 2 + 1))
                if g == 0:
                    pe.wait_ge(z6, q + 1)
                for j in range(GROUPS[g]):
                    jb = START[g] + j
                    last = pe.matmul(banks[:, q % 2, 0:D + 2], st[g % RING][:, j * P:(j + 1) * P], nf[:, jb, 0:D + 2],
                                     start=(jb == 0), stop=(jb == NB - 1))
                last.then_inc(s_used, 1)

            def steps6(q, first, last):
                for g in range(NG):
                    if g + AHEAD < NG:
                        forms(q, g + AHEAD)
                    elif not last:
                        forms(q + 1, g + AHEAD - NG)
                    if g == 4 and not first:
                        turn6(q - 1)
                    if g == 7 and not first:
                        out6(q - 1)
                    aggregate(q, g)

            with pe.If(fast != 0):
                pe.wait_ge(ft_c, RING + 2 * NT)
                for g in range(AHEAD):
                    forms(0, g)
                steps6(0, True, False)
                with pe.Fori(1, NB - 1) as q:
                    steps6(q, False, False)
                steps6(NB - 1, False, True)
                turn6(NB - 1)
                out6(NB - 1)
            with pe.Else():
                pe.wait_ge(nv2, 1)
                turn_features(nv, 2 * NT)
                pe.wait_ge(ft_c, RING + 3 * NT)
                with pe.Fori(0, NB) as q:
                    col = (q + HB) % NB
                    for g in range(HB):
                        pe.wait_ge(t_rdy, q * HB + (RING + g))
                        for dst, src in ((4, vt), (5, vt2)):
                            for j in range(2):
                                jb = 2 * g + j
                                last = pe.matmul(banks[:, dst, j * P:(j + 1) * P], ut[:, jb * P:(jb + 1) * P],
                                                 src.rearrange("p (b i) -> p b i", i=P)[:, col, :], start=True, stop=True)
                        last.then_inc(g_done, 1)
                        pe.wait_ge(t_rdy, q * HB + (RING + g + 1))
                        if g == 0:
                            pe.wait_ge(z6, q + 1)
                        for j in range(2):
                            jb = 2 * g + j
                            last = pe.matmul(banks[:, q % 2, 0:D + 2], st[3][:, j * P:(j + 1) * P], nf[:, jb, 0:D + 2],
                                             start=(jb == 0), stop=(jb == NB - 1))
                        last.then_inc(s_used, 1)
                    turn6(q)
                    out6(q)

        @block.scalar
        def _(act):
            for b in range(0, NB, 2):
                act.wait_ge(u_ps, b + 1)
                act.wait_ge(u_sb, b + 1)
                act.copy(u_all[:, :, b, :], banks[:, b % PB, 0:4 * D].rearrange("p (u c) -> p u c", u=4)).then_inc(u_sb, 1)

            def early_half(p, src, h):
                act.wait_ge(prod, NB * (p + 1))
                act.copy(moving_h[:, h, :, 0:D], src[:, h, :, :]).then_inc(m_ready, 1)

            act.wait_ge(freed, LAG + HB)
            early_half(0, halves(XW2), 0)
            act.wait_ge(freed, LAG + NB + HB)
            early_half(1, halves(XW1), 1)
            with act.Fori(0, 2) as k:
                act.wait_ge(ve, k + 1)
                act.activation(small[:, 3, 0:HB], small[:, 2, 0:HB], ACT.Sqrt).then_inc(rt, 1)
            act.wait_ge(ln_c, LN_STEPS)
            early_half(2, halves(X1), 0)

            def copy4(n, s):
                act.wait_ge(t4, n + 3)
                act.wait_ge(o4, n + (2 if s == 0 else 1))
                act.copy(zxt[:, s % 2, :], banks[:, 5, 0:P]).then_inc(c4, 1)

            def tanh4(n, s):
                act.wait_ge(h4, n + 1)
                act.activation(ht[:, s % 2, :], banks[:, 6, 0:P], ACT.Tanh, bias=hbias).then_inc(a4, 1)

            with act.Fori(0, 2) as k:
                for s in range(HB + 1):
                    if s < HB:
                        copy4(k * HB + s, s)
                    if s >= 1:
                        tanh4(k * HB + (s - 1), s - 1)
                act.wait_ge(ve, k + 3)
                act.activation(small[:, 3, 0:HB], small[:, 2, 0:HB], ACT.Sqrt).then_inc(rt, 1)

            def weights(q, g):
                act.wait_ge(c_done, q * NG + (g + 1))
                act.wait_ge(w_used, q * NG + (g + 1))
                w = GROUPS[g] * P
                act.activation(wt[g % RING].bitcast(U16)[:, 0:w], banks[:, 4 + g % RING, 0:w], ACT.Relu,
                               bias=cols[:, 11:12]).then_inc(w_rdy, 1)

            def copy5(q):
                act.wait_ge(t5, q + 1)
                act.mul(aggt5, banks[0:D, 2, 0:P], UNSCALE).then_inc(c5, 1)

            def weights_all(q, first):
                for g in range(NG):
                    weights(q, g)
                    if g == 3 and not first:
                        copy5(q - 1)

            weights_all(0, True)
            with act.Fori(1, NB) as q:
                weights_all(q, False)
            copy5(NB - 1)
            act.wait_ge(ve, 5)
            act.activation(small[:, 3, :], small[:, 2, :], ACT.Sqrt).then_inc(rt, 1)

            NT = (NB + 3) // 4

            def copy_features(dst, base):
                for t in range(NT):
                    w = min(4, NB - 4 * t) * P
                    act.wait_ge(ft_t, base + t + 1)
                    act.copy(dst[:, 4 * t * P:4 * t * P + w], banks[0:NF, 4 + (base + t) % RING, 0:w]).then_inc(ft_c, 1)

            copy_features(ut, 0)
            copy_features(vt, NT)
            act.wait_ge(fl_i, 1)
            fast = act.value_load(flag_i[0:1, 0:1], min_val=0, max_val=1)

            def copy6(q):
                act.wait_ge(t6, q + 1)
                act.copy(aggt6, banks[0:D, 2, 0:P]).then_inc(c6, 1)

            def squares(q, first):
                for g in range(NG):
                    w = GROUPS[g] * P
                    act.wait_ge(g_done, q * NG + (g + 1))
                    act.wait_ge(t_rdy, q * NG + (g + RING - 1))
                    act.activation(sq[g % 2][:, 0:w], banks[:, 4 + g % RING, 0:w], ACT.Square,
                                   bias=cols[:, 10:11]).then_inc(q_done, 1)
                    if g == 5 and not first:
                        copy6(q - 1)

            with act.If(fast != 0):
                squares(0, True)
                with act.Fori(1, NB) as q:
                    squares(q, False)
                copy6(NB - 1)
            with act.Else():
                copy_features(vt2, 2 * NT)
                with act.Fori(0, NB) as q:
                    with act.Fori(0, HB) as g:
                        it = q * HB + g
                        act.wait_ge(gv, 2 * it + 1)
                        act.activation(gen[3], gen[2], ACT.Sqrt).then_inc(ga, 1)
                        act.wait_ge(gv, 2 * it + 2)
                        act.activation(gen[5], gen[4], ACT.Ln, bias=1.0, scale=1.0)
                        act.activation(gen[6], gen[4], ACT.Ln, bias=1.0, scale=-1.0).then_inc(ga, 1)
                    copy6(q)
            act.wait_ge(vr, 1)
            act.activation(small[:, 1, :], small[:, 0, :], ACT.Sqrt).then_inc(th, 1)
            act.wait_ge(vr, 2)
            act.activation(small[:, 5, :], small[:, 4, :], ACT.Tanh).then_inc(th, 1)
            act.wait_ge(ve, 6)
            act.activation(small[:, 3, :], small[:, 2, :], ACT.Sqrt).then_inc(rt, 1)

        @block.vector
        def _(dve):
            linked = [0]

            def chain(ins):
                linked[0] += 1
                ins.then_inc(link, 1)
                dve.wait_ge(link, linked[0])

            dve.sem_inc(freed, LAG)
            dve.sem_inc(t4, 2)
            dve.sem_inc(c4, 1)
            dve.sem_inc(a4, 1)
            dve.sem_inc(o4, 2)
            dve.sem_inc(y4, 1)
            dve.sem_inc(w_rdy, W_CREDIT)
            dve.sem_inc(w_used, RING)
            dve.sem_inc(z5, 2)
            dve.sem_inc(y5, 1)
            dve.sem_inc(ft_c, RING)
            dve.sem_inc(t_rdy, RING)
            dve.sem_inc(s_used, RING)
            dve.sem_inc(z6, 2)
            dve.sem_inc(y6, 1)
            dve.sem_inc(u_sb, 1)
            chain(dve.memset(cols[:, 11:12], MASK_BIAS))
            chain(dve.memset(agg_wide[:, D:P], 0.0))
            chain(dve.memset(cols[:, 10:11], ROOT - MID))
            dve.wait_ge(c_ld, 32)
            chain(dve.tensor_scalar(hbias, const("w1t"), const("tcol"), const("b1"), ALU.mult, ALU.add))

            for b in range(1, NB, 2):
                dve.wait_ge(u_ps, b + 1)
                dve.wait_ge(u_sb, b + 1)
                dve.tensor_copy(u_all[:, :, b, :], banks[:, b % PB, 0:4 * D].rearrange("p (u c) -> p u c", u=4)).then_inc(u_sb, 1)
            dve.wait_ge(u_sb, NB + 1)
            chain(dve.memset(moving[:, :, D:D + 1], 1.0))
            dve.tensor_scalar(moving[:, :, 0:D], blocks(XW3), 2.0, None, ALU.mult).then_inc(m_ready, 2)
            dve.tensor_scalar(region(XW2), region(XW2), 2.0, None, ALU.mult)
            chain(dve.tensor_tensor(region(XW1), region(XW1), region(XW3), ALU.subtract))

            with dve.Fori(0, 2) as k:
                for s in range(HB):
                    dve.wait_ge(prod, k * HB + (s + 1))
                    o = halves(XW2)[:, k, s, :]
                    dve.tensor_scalar(neg_rs[:, :].rearrange("p (h s) -> p h s", h=2)[:, k, s:s + 1],
                                      banks[:, s % PB, D:D + 1], -1.0, None, ALU.mult)
                    dve.scalar_tensor_tensor(o, banks[:, s % PB, 0:D], 2.0, o, ALU.mult, ALU.add).then_inc(freed, 1)
            dve.wait_ge(freed, LAG + NB)
            dve.tensor_copy(moving_h[:, 1, :, 0:D], halves(XW2)[:, 1, :, :]).then_inc(m_ready, 1)
            chain(dve.scalar_tensor_tensor(region(XW0), region(XW2), -0.5, region(XW0), ALU.mult, ALU.add))

            with dve.Fori(0, 2) as k:
                for s in range(HB):
                    dve.wait_ge(prod, k * HB + (NB + s + 1))
                    o = halves(XW1)[:, (k + 1) % 2, s, :]
                    dve.tensor_tensor(o, banks[:, s % PB, 0:D], o, ALU.add).then_inc(freed, 1)
            dve.wait_ge(freed, LAG + 2 * NB)
            dve.tensor_copy(moving_h[:, 0, :, 0:D], halves(XW1)[:, 0, :, :]).then_inc(m_ready, 1)

            def norm(y, x, base, nb, turn, roots):
                n = [0]

                def step(ins):
                    n[0] += 1
                    ins.then_inc(ln_c, 1)
                    dve.wait_ge(ln_c, base + n[0])

                def col(i):
                    return stats[:, 0:nb, i]

                mean, dif, var, std, rec = (small[:, i, 0:nb] for i in (0, 1, 2, 3, 4))
                dve.tensor_tensor(mean, col(1), col(4), ALU.add)
                dve.tensor_tensor(dif, col(1), col(4), ALU.subtract)
                step(dve.tensor_tensor(var, col(2), col(5), ALU.add))
                step(dve.tensor_scalar(mean, mean, 0.5, None, ALU.mult))
                step(dve.tensor_tensor(dif, dif, dif, ALU.mult))
                step(dve.scalar_tensor_tensor(var, dif, D / 4.0, var, ALU.mult, ALU.add))
                step(dve.tensor_scalar(var, var, 0.25 / D, EPS / 4, ALU.mult, ALU.add))
                dve.sem_inc(ve, 1)
                dve.wait_ge(rt, roots + 1)
                step(dve.reciprocal(rec, std))
                step(dve.tensor_tensor(rec, rec, var, ALU.mult))
                step(dve.tensor_tensor(std, std, rec, ALU.add))
                step(dve.reciprocal(rec, std))
                step(dve.tensor_tensor(x, y, mean.unsqueeze(2).to_broadcast([P, nb, D]), ALU.subtract))
                step(dve.tensor_tensor(x, x, rec.unsqueeze(2).to_broadcast([P, nb, D]), ALU.mult))
                assert n[0] == LN_STEPS

            with dve.Fori(0, 2) as k:
                for s in range(HB + 1):
                    n = k * HB + (2 * NB + s)
                    dve.wait_ge(freed, n + LAG)
                    if s < HB:
                        dve.wait_ge(prod, n + 1)
                        o = halves(XW0)[:, k, s, :]
                        dve.tensor_tensor(o, banks[:, s % PB, 0:D], o, ALU.add).then_inc(freed, 1)
                    else:
                        dve.tensor_copy(cols[:, 8:9], hbias)
                    if s:
                        dve.bn_stats(stats[:, s - 1, :], halves(XW0)[:, k, s - 1, :]).then_inc(link, 1)
                dve.wait_ge(link, linked[0] + k * HB + HB)
                norm(halves(XW0)[:, k, :, :], halves(X1)[:, k, :, :], k * LN_STEPS, HB, k, k)
            linked[0] += NB
            dve.tensor_copy(moving_h[:, 1, :, 0:D], halves(X1)[:, 1, :, :]).then_inc(m_ready, 1)

            def z4(k, s):
                n = k * HB + s
                h = (k + 1) % 2
                dve.wait_ge(prod, n + (3 * NB + 1))
                dve.wait_ge(t4, n + (2 if s == 0 else 1))
                x = halves(X1)[:, h, s, :]
                dve.tensor_copy(zx[:, s % 2, D:2 * D], x)
                dve.scalar_tensor_tensor(zx[:, s % 2, 0:D], x,
                                         neg_rs[:, :].rearrange("p (h s) -> p h s", h=2)[:, h, s:s + 1],
                                         banks[:, s % PB, 0:D], ALU.mult, ALU.add).then_inc(freed, 1)

            def y4_read(k, s):
                n = k * HB + s
                dve.wait_ge(o4, n + 3)
                o = halves(Y1)[:, (k + 1) % 2, s, :]
                dve.tensor_copy(o, banks[:, 7, 0:D]).then_inc(y4, 1)

            with dve.Fori(0, 2) as k:
                for s in range(HB + 4):
                    if s < HB:
                        z4(k, s)
                    if s >= 4:
                        y4_read(k, s - 4)
                for s in range(HB):
                    if s == 0:
                        dve.wait_ge(y4, k * HB + (HB + 1))
                        dve.tensor_copy(cols[:, 8:9], hbias)
                    dve.bn_stats(stats[:, s, :], halves(Y1)[:, (k + 1) % 2, s, :]).then_inc(link, 1)
                dve.wait_ge(link, linked[0] + k * HB + HB)
                norm(halves(Y1)[:, (k + 1) % 2, :, :], halves(X2)[:, (k + 1) % 2, :, :], k * LN_STEPS + 2 * LN_STEPS, HB, k, k + 2)
            linked[0] += NB
            x2 = blocks(X2)
            rest = blocks(Y1)
            chain(dve.tensor_copy(spl[:, :, 0, :], x2))
            chain(dve.tensor_tensor(rest, x2, spl[:, :, 0, :], ALU.subtract))
            chain(dve.tensor_copy(spl[:, :, 1, :], rest))
            dve.tensor_tensor(spl[:, :, 2, :], rest, spl[:, :, 1, :], ALU.subtract).then_inc(spl_rdy, 1)

            chain(dve.memset(ci_buf[0][:, NB * P:(NB + 1) * P], 0.0))
            dve.wait_ge(spl_rdy, 1)
            chain(dve.memset(ci_buf[1][:, NB * P:(NB + 1) * P], 0.0))

            def masks(q, buf, last_out=None):
                dve.wait_ge(arrived, q + (4 * HB + 1))
                dve.wait_ge(w_rdy, q * NG + RING)
                c = ci_buf[buf]
                for n, j in enumerate(reversed(range(NB))):
                    if n:
                        dve.wait_ge(ci, q * NB + n)
                    dve.scalar_tensor_tensor(c[:, j * P:(j + 1) * P], a_slot[:, q % HB, j, :], 0.0,
                                             c[:, (j + 1) * P:(j + 2) * P], ALU.not_equal, ALU.add).then_inc(ci, 1)
                    if last_out is not None and n == NB - 3:
                        read5(last_out)

            def sum5(q, bank):
                dve.wait_ge(w_used, q * NG + (RING + NG))
                dve.tensor_reduce(agg[:, :], banks[:, bank, 0:3 * D].rearrange("p (k c) -> p c k", k=3), AX_X, ALU.add)\
                    .then_inc(z5, 1)

            def read5(q):
                dve.wait_ge(o5, q + 1)
                o = x2[:, q, :]
                dve.tensor_tensor(o, banks[:, 3, 0:D], o, ALU.add).then_inc(y5, 1)

            masks(0, 0)
            masks(1, 1)
            with dve.Fori(0, HB - 1) as h:
                for t in range(2):
                    q = 2 * h + t
                    sum5(q, t)
                    masks(q + 2, t, q)
            for q in (NB - 2, NB - 1):
                sum5(q, q % 2)
                read5(q)
            dve.wait_ge(y5, NB + 1)
            for b in range(NB):
                last = dve.bn_stats(stats[:, b, :], x2[:, b, :])
            chain(last)
            norm(x2, x3, 4 * LN_STEPS, NB, 0, 4)

            nrm, bb, dev, mm, deg, beta, g1, bg1 = (small[:, i, :] for i in (0, 1, 2, 3, 4, 5, 6, 7))
            sqv = v3
            chain(dve.tensor_tensor(sqv, x3, x3, ALU.mult))
            chain(dve.tensor_reduce(nrm, sqv, AX_X, ALU.add))
            dve.tensor_scalar(bb, nrm, -1.0, 1.0, ALU.mult, ALU.add)
            chain(dve.tensor_scalar(dev, nrm, -float(D), None, ALU.add))
            chain(dve.scalar_tensor_tensor(dev, dev, -1.0, dev, ALU.mult, ALU.max))
            chain(dve.tensor_tensor(dev[:, NB - 1:NB], dev[:, NB - 1:NB], const("valid"), ALU.mult))
            dve.tensor_reduce(cols[:, 0:1], dev, AX_X, ALU.max).then_inc(pm_t, 1)
            dve.tensor_scalar(mm, bb, MIN_NORM, None, ALU.max)
            chain(dve.tensor_scalar(deg, neg_rs[:, :], -1.0, 1e-8, ALU.mult, ALU.max))
            chain(dve.reciprocal(deg, deg))
            chain(dve.tensor_tensor(g1, mm, deg, ALU.mult))
            dve.wait_ge(pm_r, 1)
            chain(dve.tensor_reduce(cols[0:1, 1:2], banks[0:1, 2, 0:P], AX_X, ALU.max))
            dve.tensor_scalar(cols[0:1, 2:3], cols[0:1, 1:2], NEAR, None, ALU.is_le).then_inc(pm_t, 1)
            dve.wait_ge(pm_t, 2)
            chain(dve.tensor_copy(flag_i[:, :], cols[0:1, 2:3]))
            dve.sem_inc(fl_i, 1)
            dve.wait_ge(fl_b, 1)
            flag = cols[:, 3:4]
            chain(dve.tensor_copy(flag, banks[:, 3, 0:1]))
            dve.tensor_scalar(cols[:, 4:5], flag, C3 - 1.0, 1.0, ALU.mult, ALU.add)
            dve.tensor_scalar(cols[:, 5:6], flag, -ROOT, None, ALU.mult)
            chain(dve.tensor_scalar(beta, bb, -1.0, flag, ALU.add, ALU.mult))
            chain(dve.tensor_scalar(beta, beta, 1.0, None, ALU.add))
            chain(dve.reciprocal(beta, beta))
            wide = beta.unsqueeze(2).to_broadcast([P, NB, D])
            dve.tensor_tensor(nf[:, :, 0:D], x3, wide, ALU.mult)
            dve.tensor_tensor(nf[:, :, D], nrm, beta, ALU.mult)
            dve.tensor_copy(nf[:, :, D + 1], beta)
            dve.memset(nf[:, :, D + 2], 1.0).then_inc(nat, 1)
            dve.wait_ge(nat, 1)
            dve.tensor_scalar(nv[:, :, 0:D], nf[:, :, 0:D], -2.0, None, ALU.mult)
            dve.tensor_copy(nv[:, :, D], beta)
            dve.tensor_copy(nv[:, :, D + 1], nf[:, :, D])
            dve.tensor_scalar(nv[:, :, D + 2], nf[:, :, D + 2], cols[:, 5:6], None, ALU.mult).then_inc(nat, 1)
            chain(dve.tensor_tensor(g1, g1, beta, ALU.mult))
            chain(dve.tensor_scalar(g1, g1, cols[:, 4:5], None, ALU.mult))
            chain(dve.tensor_tensor(bg1, bb, g1, ALU.mult))
            fast = dve.value_load(flag_i[0:1, 0:1], min_val=0, max_val=1)

            def gather6(q, count, base):
                def step(ins, n):
                    ins.then_inc(gl, 1)
                    dve.wait_ge(gl, base + n)

                idx = (q + HB) % NB
                o = banks[:, q % 2, :]
                x = x3[:, idx, :]
                dve.wait_ge(s_used, count)
                step(dve.tensor_tensor(agg[:, :], o[:, 0:D], x, ALU.mult), 1)
                step(dve.tensor_reduce(cols[:, 6:7], agg[:, :], AX_X, ALU.add), 2)
                step(dve.tensor_scalar(cols[:, 6:7], cols[:, 6:7], -2.0, o[:, D:D + 1], ALU.mult, ALU.add), 3)
                step(dve.tensor_scalar(cols[:, 7:8], cols[:, 6:7], o[:, D + 1:D + 2], g1[:, bass.ds(idx, 1)], ALU.add, ALU.mult), 4)
                step(dve.tensor_scalar(agg[:, :], x, cols[:, 7:8], None, ALU.mult), 5)
                dve.scalar_tensor_tensor(agg[:, :], o[:, 0:D], bg1[:, bass.ds(idx, 1)], agg[:, :], ALU.mult, ALU.subtract)\
                    .then_inc(z6, 1)

            def read6(q):
                dve.wait_ge(o6, q + 1)
                dve.tensor_copy(v3[:, (q + HB) % NB, :], banks[:, 3, 0:D]).then_inc(y6, 1)

            GATHER = 5

            def shape6(q, g):
                w = GROUPS[g] * P
                dve.wait_ge(q_done, q * NG + (g + 1))
                dve.wait_ge(s_used, q * NG + (g + 1))
                dve.scalar_tensor_tensor(st[g % RING][:, 0:w], sq[g % 2][:, 0:w], FAR, banks[:, 4 + g % RING, 0:w],
                                         ALU.add, ALU.mult).then_inc(t_rdy, 1)

            def times_a(q, g):
                j0, w = START[g], GROUPS[g] * P
                s = st[g % RING][:, 0:w]
                dve.wait_ge(t_rdy, q * NG + (RING + g + 1))
                ins = dve.tensor_tensor(s, s, a_flat[:, q % SLOTS6, j0 * P:j0 * P + w], ALU.mult)
                ins.then_inc(sd_rdy, 1)

            def steps6(q, first):
                dve.wait_ge(arrived, q + (5 * HB + 5))
                for g in range(NG):
                    shape6(q, g)
                    if g % 2:
                        times_a(q, g)
                    if g == 3 and not first:
                        dve.wait_ge(sd_rdy, q * (NG // 2))
                        dve.wait_ge(sp_rdy, q * (NG // 2))
                        dve.sem_inc(a_used, 1)
                        gather6(q - 1, q * NG + RING, q * GATHER - GATHER)
                    if g == 7 and not first:
                        read6(q - 1)

            with dve.If(fast != 0):
                steps6(0, True)
                with dve.Fori(1, NB) as q:
                    steps6(q, False)
                gather6(NB - 1, NB * NG + RING, (NB - 1) * GATHER)
                read6(NB - 1)
            with dve.Else():
                dve.wait_ge(ft_c, RING + 2 * ((NB + 3) // 4))
                dve.tensor_copy(nv[:, :, D], nf[:, :, D])
                dve.tensor_copy(nv[:, :, D + 1], nf[:, :, D + 1]).then_inc(nv2, 1)
                KG = 24
                with dve.Fori(0, NB) as q:
                    with dve.Fori(0, HB) as g:
                        it = q * HB + g
                        dve.wait_ge(arrived, q + (5 * HB + 5))
                        n = [0]

                        def step(ins):
                            n[0] += 1
                            ins.then_inc(gl, 1)
                            dve.wait_ge(gl, it * KG + q * GATHER + n[0])

                        dm, rec, r, root, z, lp, lm, f, qq, mask, tmp = gen
                        den, d2 = banks[:, 5, 0:256], banks[:, 4, 0:256]
                        dve.wait_ge(g_done, it + 1)
                        step(dve.tensor_scalar(dm, den, MIN_NORM, None, ALU.max))
                        step(dve.reciprocal(rec, dm))
                        step(dve.scalar_tensor_tensor(r, d2, 0.0, rec, ALU.max, ALU.mult))
                        step(dve.tensor_scalar(r, r, MIN_NORM * MIN_NORM, None, ALU.max))
                        dve.sem_inc(gv, 1)
                        dve.wait_ge(ga, 2 * it + 1)
                        step(dve.tensor_scalar(z, root, TANH_CLIP, None, ALU.min))
                        dve.sem_inc(gv, 1)
                        step(dve.tensor_scalar(qq, r, SMALL, None, ALU.min))
                        step(dve.tensor_scalar(mask, r, SMALL, None, ALU.is_gt))
                        step(dve.tensor_scalar(f, qq, 1 / 13, SERIES[0], ALU.mult, ALU.add))
                        for c in SERIES[1:]:
                            step(dve.tensor_tensor(f, f, qq, ALU.mult))
                            step(dve.tensor_scalar(f, f, c, None, ALU.add))
                        step(dve.reciprocal(tmp, root))
                        dve.wait_ge(ga, 2 * it + 2)
                        step(dve.tensor_tensor(lp, lp, lm, ALU.subtract))
                        step(dve.scalar_tensor_tensor(lp, lp, 0.5, tmp, ALU.mult, ALU.mult))
                        step(dve.tensor_tensor(lp, lp, mask, ALU.mult))
                        step(dve.tensor_scalar(mask, mask, -1.0, 1.0, ALU.mult, ALU.add))
                        step(dve.tensor_tensor(f, f, mask, ALU.mult))
                        assert n[0] == KG, n[0]
                        dve.tensor_tensor(f, f, lp, ALU.add).then_inc(gen_f, 1)
                        dve.wait_ge(gen_f, 2 * it + 1)
                        dve.tensor_tensor(f, f, rec, ALU.mult).then_inc(gen_f, 1)
                        dve.wait_ge(gen_f, 2 * it + 2)
                        dve.wait_ge(s_used, it + RING)
                        dve.tensor_tensor(st[3][:, 0:256], f,
                                          slots[:, :].rearrange("p (s g w) -> p s g w", s=HB, g=HB)[:, q % SLOTS6, g, :],
                                          ALU.mult).then_inc(t_rdy, 1)
                    dve.wait_ge(t_rdy, q * HB + (RING + HB))
                    dve.sem_inc(a_used, 1)
                    gather6(q, q * HB + (RING + HB), q * (HB * KG + GATHER) + HB * KG)
                    read6(q)

            dve.wait_ge(y6, 1 + NB)
            sqo = nf[:, :, 0:D]
            ss, root, rec, vn, tanh = (small[:, i, :] for i in (0, 1, 2, 4, 5))
            dve.tensor_tensor(sqo, v3, v3, ALU.mult).then_inc(fin, 1)
            dve.wait_ge(fin, 1)
            dve.tensor_reduce(ss, sqo, AX_X, ALU.add).then_inc(vr, 1)
            dve.wait_ge(th, 1)
            nf_ = [1]

            def fstep(ins):
                nf_[0] += 1
                ins.then_inc(fin, 1)
                dve.wait_ge(fin, nf_[0])

            fstep(dve.tensor_scalar(root, root, MIN_NORM, None, ALU.max))
            fstep(dve.reciprocal(rec, root))
            fstep(dve.tensor_tensor(rec, rec, ss, ALU.mult))
            fstep(dve.tensor_tensor(vn, rec, root, ALU.add))
            fstep(dve.tensor_scalar(vn, vn, 0.5, MIN_NORM, ALU.mult, ALU.max))
            dve.sem_inc(vr, 1)
            fstep(dve.reciprocal(rec, vn))
            dve.wait_ge(th, 2)
            fstep(dve.tensor_tensor(rec, rec, tanh, ALU.mult))
            fstep(dve.tensor_tensor(v3, v3, rec.unsqueeze(2).to_broadcast([P, NB, D]), ALU.mult))
            fstep(dve.tensor_tensor(v3, v3, x3, ALU.add))
            for b in range(NB):
                last = dve.bn_stats(stats[:, b, :], v3[:, b, :])
            fstep(last)
            norm(v3, v3, 5 * LN_STEPS, NB, 0, 5)
            dve.sem_inc(y6, 1)


LN_STEPS = 11


def kernel(**inputs):
    import numpy as np
    import ml_dtypes
    import concourse.bacc as _bacc
    from concourse import mybir as _mybir
    from concourse.bass_utils import run_bass_kernel_spmd as _run

    g = {k: np.ascontiguousarray(v) for k, v in inputs.items()}
    f32 = np.float32
    adj = np.zeros((NP, NP), f32)
    adj[:N, :N] = g["adj"]
    a_blocks = np.ascontiguousarray(adj.reshape(NB, P, NB, P).transpose(0, 3, 2, 1)).reshape(NB, P, NB * P)
    xt = np.zeros((D + 1, NP), f32)
    xt[:D, :N] = g["x"].T
    xt[D] = 1.0
    w = g["L0_gnn_weights"]
    wcat = np.zeros((D + 1, 4 * D), f32)
    for i, k in enumerate((3, 2, 1, 0)):
        wcat[:D, i * D:(i + 1) * D] = w[k]
    wcat[D, 3 * D:] = g["L0_gnn_bias"]
    consts = np.zeros((P, NCONST), f32)

    def put(name, a, row=0):
        consts[row:row + a.shape[0], COLS[name][0]:COLS[name][1]] = a

    put("ident", np.eye(P, dtype=f32))
    put("bt", g["L1_gnn_B"].T)
    put("bt", np.eye(D, dtype=f32), D)
    put("w1", g["L1_gnn_W1"][:D], D)
    put("w2", g["L1_gnn_W2"])
    put("lw2", g["L2_gnn_weight"])
    put("lw3", g["L3_gnn_weight"])
    for name, key in (("b2", "L1_gnn_b2"), ("lb2", "L2_gnn_bias"), ("lb3", "L3_gnn_bias")):
        put("bias", g[key][None], BIAS_ROW[name])
        put("ones", np.ones((1, P), f32), BIAS_ROW[name])
    put("tcol", np.repeat(g["L1_gnn_t"][None], P, 0))
    put("w1t", g["L1_gnn_W1"][D][:, None])
    put("b1", g["L1_gnn_b1"][:, None])
    put("valid", (np.arange(P) < N - (NB - 1) * P).astype(f32)[:, None])
    k, j = np.indices((P, P))
    t0 = np.where(k > j, -UNIT, 0) + np.where(k == j, UNIT * DIAG, 0)
    t1 = -UNIT - t0
    tri = np.stack([t0, t1], 1).astype(ml_dtypes.bfloat16)

    nc = _bacc.Bacc("TRN2", target_bir_lowering=False, num_devices=1)
    arrays = {"a_blocks": a_blocks, "xt": xt, "wcat": wcat, "consts": consts, "tri": tri}
    args = [nc.dram_tensor(n, a.shape, _mybir.dt.from_np(a.dtype), kind="ExternalInput").ap() for n, a in arrays.items()]
    args.append(nc.dram_tensor("out", (N, D), _mybir.dt.float32, kind="ExternalOutput").ap())
    gnn_kernel(nc, *args)
    r = _run(nc, [arrays], core_ids=[0])
    return r.results[0]["out"]
```

```python
import struct
from contextlib import ExitStack

import concourse.bass as bass
from concourse import mybir

F32 = mybir.dt.float32
BF16 = mybir.dt.bfloat16
U16 = mybir.dt.uint16
I32 = mybir.dt.int32
ALU = mybir.AluOpType
ACT = mybir.ActivationFunctionType
AX_X = mybir.AxisListType.X

P = 128
N = 3327
D = 64
NB = (N + P - 1) // P
NP = NB * P
HB = NB // 2
EPS = 1e-5

CHUNKS = [(0, 4), (4, 3), (7, 3), (10, 3)]
NC = len(CHUNKS)
PAIRS = NB // 2
assert sum(c for _, c in CHUNKS) == HB and NB % 2 == 0

CUT = 100
UNIT = 128
DIAG = 128
MASK_BIAS = float(UNIT * CUT - UNIT * DIAG)
UNSCALE = 2.0 ** 27

NEAR = 0.5
ROOT = 1.39459825
MID = -0.04442543
FAR = 1.32681359 ** 2
C3 = -0.40685946
TANH_CLIP = 1.0 - 1e-5
MIN_NORM = 1e-15
SMALL = 0.0625
SERIES = [1 / 11, 1 / 9, 1 / 7, 1 / 5, 1 / 3, 1.0]

COLS = {}
_at = 0
for _name, _w in (("ident", P), ("fold", D), ("bt", D), ("qb", D), ("w1", P), ("w2", D), ("lw2", D), ("lw3", D),
                  ("b2", D), ("lb2", D), ("lb3", D), ("tcol", 1), ("w1t", 1), ("b1", 1), ("valid", 1), ("one", 1)):
    COLS[_name] = (_at, _at + _w)
    _at += _w
NCONST = _at

SLOT = NB * P
STEP6 = 4
SLOTS6 = 8
FULL6 = NB // STEP6
REST6 = NB - FULL6 * STEP6
NF = D + 3
KA, KB = 2 * D, D + 16
RING = 4
LN_STEPS = 11


FIN_ALL = 13
RS_RING = 5


def rs_buf(s):
    return s % RS_RING


def rs_gap(s):
    return RS_RING if s >= RS_RING else next(d for d in range(1, HB + 1) if (s - d) % HB % RS_RING == s)


def bf16_parts(v):
    parts = []
    for _ in range(3):
        u = struct.unpack("<I", struct.pack("<f", v))[0]
        u = (u + 0x7FFF + ((u >> 16) & 1)) & 0xFFFF0000
        parts.append(struct.unpack("<f", struct.pack("<I", u))[0])
        v -= parts[-1]
    return parts


ROOT_PARTS = bf16_parts(struct.unpack("<f", struct.pack("<f", ROOT))[0])


def gnn_kernel(nc, a_blocks, xt, wcat, consts, tri, out):
    with ExitStack() as ctx:
        def sb(name, shape, dt=F32):
            return ctx.enter_context(nc.sbuf_tensor(name, shape, dt))

        def sem(name):
            return ctx.enter_context(nc.semaphore(name))

        slots = sb("slots", [P, HB * SLOT])
        REGION = NB * D
        work = sb("work", [P, 5 * REGION])
        cst = sb("cst", [P, NCONST])
        tri_sb = sb("tri_sb", [P, 3, P], BF16)
        stats = sb("stats", [P, NB, 6])
        small = sb("small", [P, 8, NB])
        cols = sb("cols", [P, 12])
        neg_rs = sb("neg_rs", [P, NB])
        flag_i = sb("flag_i", [1, 1], I32)
        banks = ctx.enter_context(nc.psum_tensor("banks", [P, 8, 512], F32))
        hbias = cols[:, 9:10]

        def const(name, rows=P):
            a, b = COLS[name]
            return cst[0:rows, a:b]

        ident = const("ident")

        a_slot = slots[:, :].rearrange("p (s j i) -> p s j i", s=HB, j=NB)
        a_flat = slots[:, :].rearrange("p (s w) -> p s w", s=HB)
        xt_sb = slots[0:D + 1, (HB - 1) * SLOT:HB * SLOT]

        def words(a, n):
            return work[:, a:a + n]

        def region(n):
            return words((n + 1) * REGION, REGION)

        def halves(n):
            return region(n).rearrange("p (h w) -> p h w", h=2)

        def rows(n, h, s0, cnt):
            return halves(n)[:, h, s0 * D:(s0 + cnt) * D]

        def blocks(n):
            return region(n).rearrange("p (b c) -> p b c", c=D)

        moving = words(0, REGION).rearrange("p (j c) -> p j c", c=D)
        moving_h = words(0, REGION).rearrange("p (h w) -> p h w", h=2)
        wcat_sb = work[0:D + 1, 0:4 * D]
        u_all = words(REGION, 4 * REGION).rearrange("p (u b c) -> p u b c", u=4, c=D)
        XW3, XW2, XW1, XW0 = 0, 1, 2, 3
        X1, Y1, X2 = 1, 2, 3
        yt = [words(REGION + 512 * n, 512) for n in range(2)]
        rsp = words(REGION + 1024, RS_RING * P).rearrange("p (b i) -> p b i", i=P)
        zx = words(2 * REGION, 512).rearrange("p (b c) -> p b c", c=P)
        zxt = words(2 * REGION + 512, 512)
        ht = words(2 * REGION + 1024, 512)
        spl_w = NB * 3 * D // 2
        spl = words(0, spl_w).bitcast(BF16).rearrange("p (j c) -> p j c", c=3 * D)
        at = spl_w
        ci_buf = [words(at + 256 * n, 256).bitcast(BF16) for n in range(RING)]
        ci_zero = words(at + 256 * RING, 256).bitcast(BF16)
        at += 256 * (RING + 1)
        wt = [words(at + 256 * n, 256).bitcast(BF16) for n in range(RING)]
        at += 256 * RING
        oh, ol = words(at, 512), words(at + 512, 512)
        assert at + 1024 <= (X2 + 1) * REGION
        nf = words(0, NB * (D + 1)).rearrange("p (b c) -> p b c", c=D + 1)
        at = NB * (D + 1)
        v3 = words(at, REGION).rearrange("p (b c) -> p b c", c=D)
        at += REGION
        ot = work[0:D + 1, at:at + 512]
        agg = words(at + 512, 4 * D).rearrange("p (b c) -> p b c", c=D)
        agg_flat = words(at + 512, 4 * D)
        tmp6 = words(at + 768, 4 * D).rearrange("p (b c) -> p b c", c=D)
        aggt = words(at + 1024, 2 * P)
        parts = words(at + 1280, 128).bitcast(BF16)[:, 0:NB * 9].rearrange("p (b c) -> p b c", c=9)
        assert at + 1408 <= (X2 + 1) * REGION
        x3 = blocks(X2)
        t8 = SLOTS6 * SLOT
        ua, ub, va, vb = (slots[0:k, t8 + n * SLOT // 2:t8 + (n + 1) * SLOT // 2].bitcast(BF16)
                          for n, k in enumerate((KA, KB, KA, KB)))
        nat_w = (KA + KB) // 2 * NB
        nu, nv = (slots[:, t8 + 2 * SLOT + n * nat_w:t8 + 2 * SLOT + (n + 1) * nat_w].bitcast(BF16)
                  .rearrange("p (b c) -> p b c", c=KA + KB) for n in range(2))
        assert 2 * nat_w <= 2 * SLOT
        st = [slots[:, t8 + 4 * SLOT + 512 * n:t8 + 4 * SLOT + 512 * (n + 1)] for n in range(RING)]
        sq = [slots[:, t8 + 4 * SLOT + 512 * n:t8 + 4 * SLOT + 512 * (n + 1)] for n in range(RING, RING + 2)]
        gen = [slots[:, t8 + 512 * n:t8 + 512 * (n + 1)] for n in range(12)]
        gen_s = gen[11]
        ut, vt, vt2 = (slots[0:NF, t8 + (2 + n) * SLOT:t8 + (3 + n) * SLOT] for n in range(3))
        gu = slots[:, t8 + 4 * SLOT:t8 + 4 * SLOT + NB * NF].rearrange("p (b c) -> p b c", c=NF)

        ld = [sem(f"slot_loaded{s}") for s in range(HB)]
        c_ld = sem("constants_loaded")
        x_ld = sem("xt_loaded")
        ld6 = sem("pass5_loaded")
        arrived = sem("blocks_arrived")
        u_ps = sem("xw_in_psum")
        u_sb = sem("xw_in_sbuf")
        m_ready = sem("moving_ready")
        prod = sem("chunk_product_done")
        y_rdy = sem("product_in_sbuf")
        bk = sem("product_turned_back")
        freed = sem("chunk_read")
        rs_sum = sem("partial_row_sums")
        rs_ps = sem("row_sums_in_psum")
        link = sem("vector_chain")
        ln_c = sem("norm_chain")
        ve = sem("variance_ready")
        rt = sem("root_ready")
        zx_r, t4, c4, h4, a4, y4 = (sem(f"comm_{n}") for n in ("features", "turned", "turned_in_sbuf", "hidden", "tanh", "read"))
        spl_rdy = sem("split_ready")
        ci = sem("suffix_masks_built")
        c_done = sem("counts_done")
        w_rdy = sem("weights_ready")
        w_used = sem("weights_used")
        c5, o5, y5 = (sem(f"decay_{n}") for n in ("sum_in_sbuf", "out", "out_read"))
        pm_t = sem("deviation_ready")
        pm_r = sem("deviation_turned")
        fl_b = sem("flag_spread")
        fl_i = sem("flag_ready")
        nat = sem("features_ready")
        ft_t = sem("features_turned")
        ft_c = sem("features_copied")
        g_done = sem("forms_done")
        q_done = sem("squares_done")
        t_rdy = sem("weights_before_a")
        sd_rdy = sem("s_ready_vector")
        sp_rdy = sem("s_ready_pool")
        s_used = sem("s_used")
        gl = sem("gather_chain")
        gc = sem("general_chain")
        ga = sem("general_act_done")
        gv = sem("general_act_input")
        e6, b6, z6, t6, c6, o6, y6 = (sem(f"ball_{n}") for n in (
            "sum_in_sbuf", "sum_turned", "agg_ready", "agg_turned", "turned_in_sbuf", "out", "out_read"))
        a_used = sem("pass5_chunk_used")
        th = sem("act_result_ready")
        vr = sem("act_input_ready")
        fin = sem("final_chain")
        stored = sem("stored")

        block = ctx.enter_context(nc.Block())

        @block.sync
        def _(sp):
            sp.dma_start(xt_sb, xt).then_inc(x_ld, 16)
            sp.dma_start(wcat_sb, wcat).then_inc(x_ld, 16)
            sp.dma_start(cst[:, :], consts).then_inc(c_ld, 16)
            sp.dma_start(tri_sb[:, :, :], tri).then_inc(c_ld, 16)
            for s in range(HB):
                if s == HB - 1:
                    sp.wait_ge(u_ps, NB)
                sp.dma_start(a_flat[:, s], a_blocks[HB + s]).then_inc(ld[s], 16)
            with sp.Fori(1, 5) as g:
                for c, (s0, cnt) in enumerate(CHUNKS):
                    for s in range(s0, s0 + cnt):
                        sp.wait_ge(prod, g * (2 * NC) + (c + 1 - 2 * NC))
                        sp.wait_ge(rs_sum, HB)
                        sp.dma_start(a_flat[:, s], a_blocks[((g + 1) % 2) * HB + s]).then_inc(ld[s], 16)
            for c, (s0, cnt) in enumerate(CHUNKS):
                for s in range(s0, s0 + cnt):
                    sp.wait_ge(ci, NB * (c + 1))
                    sp.dma_start(a_flat[:, s], a_blocks[s]).then_inc(ld[s], 16)
            wide = slots[:, 0:SLOTS6 * SLOT].rearrange("p (t w) -> p t w", t=2)
            with sp.Fori(2, FULL6) as t:
                sp.wait_ge(a_used, t - 1)
                src = a_blocks[0:FULL6 * STEP6].rearrange("(t b) p w -> t p b w", b=STEP6)
                sp.dma_start(wide[:, t % 2].rearrange("p (b w) -> p b w", b=STEP6), src[t]).then_inc(ld6, 16)
                sp.wait_ge(ld6, 16 * t - 16)
                sp.sem_inc(arrived, 1)
            sp.wait_ge(a_used, FULL6 - 1)
            sp.dma_start(a_flat[:, 0:REST6, :] if FULL6 % 2 == 0 else a_flat[:, STEP6:STEP6 + REST6, :],
                         a_blocks[FULL6 * STEP6:NB].rearrange("b p w -> p b w")).then_inc(ld6, 16)
            sp.wait_ge(ld6, 16 * (FULL6 - 1))
            sp.sem_inc(arrived, 1)
            sp.wait_ge(fin, FIN_ALL)
            full = N // P
            sp.dma_start(out[0:full * P].rearrange("(b p) c -> p b c", p=P), v3[:, 0:full, :]).then_inc(stored, 16)
            sp.dma_start(out[full * P:N], v3[0:N - full * P, full, :]).then_inc(stored, 16)
            sp.wait_ge(stored, 32)

        def a6(t, jb, cnt):
            if isinstance(t, int):
                s0 = (t % 2) * STEP6
                return a_slot[:, s0:s0 + cnt, jb, :]
            return slots[:, 0:SLOTS6 * SLOT].rearrange("p (t b j i) -> p t b j i", t=2, b=STEP6, j=NB)[:, t % 2, :, jb, :]

        def out6_ps(odd, n):
            return banks[:, 3 - odd, 320:320 + n * D].rearrange("p (b c) -> p b c", c=D)

        def split(ap, cnt):
            return ap[:, 0:cnt * P].rearrange("p (b i) -> p b i", i=P)

        def over_chunks(eng, body):
            body(0, STEP6, True, STEP6)
            with eng.Fori(1, FULL6 - 1) as t:
                body(t, STEP6, False, STEP6)
            body(FULL6 - 1, STEP6, False, REST6)
            body(FULL6, REST6, False, 0)

        @block.gpsimd
        def _(pool):
            with pool.Fori(0, 6) as g:
                for s in range(HB):
                    pool.wait_ge(ld[s], 16 * g + 16)
                    pool.sem_inc(arrived, 1)
            pool.wait_ge(fl_i, 1)
            fast = pool.value_load(flag_i[0:1, 0:1], min_val=0, max_val=1)

            def even_blocks(t, cnt, first, nxt):
                for jb in range(0, NB, 2):
                    pool.wait_ge(arrived, t + (6 * HB - 1))
                    pool.wait_ge(t_rdy, t * NB + (RING + jb + 1))
                    s = split(st[jb % RING], cnt)
                    nc.gpsimd.tensor_tensor(s, s, a6(t, jb, cnt), ALU.mult).then_inc(sp_rdy, 1)

            with pool.If(fast != 0):
                over_chunks(pool, even_blocks)
            with pool.Else():
                pool.wait_ge(fl_i, 1)

        @block.tensor
        def _(pe):
            pe.wait_ge(x_ld, 32)
            pe.wait_ge(c_ld, 32)
            for b in range(NB):
                if b >= RING:
                    pe.wait_ge(u_sb, b - RING + 2)
                o = banks[:, b % RING, 0:4 * D]
                pe.matmul(o, xt_sb[:, b * P:(b + 1) * P], wcat_sb, start=True, stop=False)
                pe.matmul(o[:, 3 * D:4 * D], xt_sb[:, b * P:(b + 1) * P], const("ident", D + 1)[:, 0:D],
                          start=False, stop=True).then_inc(u_ps, 1)

            def product(n, c, k_arrived, between):
                s0, cnt = CHUNKS[c]
                pe.wait_ge(arrived, k_arrived + (s0 + cnt))
                pe.wait_ge(y_rdy, n + 1)
                for h in range(PAIRS):
                    if h in between:
                        between[h]()
                    for side in range(2):
                        j = 2 * h + side
                        last = pe.matmul(banks[side * D:(side + 1) * D, c % 2, 0:cnt * P], moving[:, j, :],
                                         a_slot[:, s0:s0 + cnt, j, :], start=(h == 0), stop=(h == PAIRS - 1))
                last.then_inc(prod, 1)

            def back(n, c):
                pe.wait_ge(y_rdy, n + 3)
                pe.wait_ge(freed, n + 1)
                for i in range(CHUNKS[c][1]):
                    last = pe.matmul(banks[:, 2 + c % 2, i * D:(i + 1) * D], yt[c % 2][:, i * P:(i + 1) * P],
                                     const("fold"), start=True, stop=True)
                last.then_inc(bk, 1)

            def row_sums(k, c):
                for s in range(CHUNKS[c][0], CHUNKS[c][0] + CHUNKS[c][1]):
                    pe.wait_ge(rs_sum, k * HB + (s + 1))
                    buf = rs_buf(s)
                    pe.matmul(banks[:, 4, s:s + 1], rsp[:, buf, :], const("one"), start=True, stop=True)\
                        .then_inc(rs_ps, 1)

            with pe.Fori(0, 2) as k:
                pe.wait_ge(m_ready, 2)
                for c in range(NC):
                    n = k * NC + c
                    product(n, c, k * HB, {4: lambda n=n, c=c: back(n - 1, c - 1)} if c else {})
                    row_sums(k, c)
                back(k * NC + (NC - 1), NC - 1)
            with pe.Fori(1, 3) as p:
                with pe.Fori(0, 2) as k:
                    pe.wait_ge(m_ready, 2 * p + 2)
                    for c in range(NC):
                        n = p * (2 * NC) + k * NC + c
                        product(n, c, p * HB + k * HB, {4: lambda n=n, c=c: back(n - 1, c - 1)} if c else {})
                    back(p * (2 * NC) + k * NC + (NC - 1), NC - 1)

            def turn4(m, c):
                pe.wait_ge(zx_r, m + 1)
                pe.wait_ge(c4, m + 1)
                for i in range(CHUNKS[c][1]):
                    last = pe.transpose(banks[:, 4, i * P:(i + 1) * P], zx[:, i, :], ident)
                last.then_inc(t4, 1)

            def hidden4(m, c):
                w = CHUNKS[c][1] * P
                pe.wait_ge(c4, m + 2)
                pe.wait_ge(a4, m + 1)
                pe.matmul(banks[:, 5, 0:w], const("w1")[D:2 * D, :], zxt[D:2 * D, 0:w], start=True, stop=True)\
                    .then_inc(h4, 1)

            def sum4(m, c):
                pe.wait_ge(y_rdy, m + (6 * NC + 3))
                pe.wait_ge(a4, m + 2)
                pe.wait_ge(y4, m + 1)
                for i in range(CHUNKS[c][1]):
                    o = banks[:, 6 + c % 2, i * D:(i + 1) * D]
                    pe.matmul(o, yt[c % 2][:, i * P:(i + 1) * P], const("bt"), start=True, stop=False)
                    pe.matmul(o, zxt[:, i * P:(i + 1) * P], const("qb"), start=False, stop=False)
                    last = pe.matmul(o, ht[:, i * P:(i + 1) * P], const("w2"), start=False, stop=True)
                last.then_inc(bk, 1)

            with pe.Fori(0, 2) as k:
                pe.wait_ge(m_ready, 8)
                for c in range(NC):
                    m = k * NC + c
                    between = {4: lambda m=m, c=c: turn4(m, c), 7: lambda m=m, c=c: hidden4(m, c)}
                    if c:
                        between[2] = lambda m=m, c=c: sum4(m - 1, c - 1)
                    product(m + 6 * NC, c, k * HB + 3 * HB, between)
                sum4(k * NC + (NC - 1), NC - 1)

            def counts(n, c, i):
                k4 = n * NB + i
                g = c * NB + i
                w = CHUNKS[c][1] * P
                pe.wait_ge(ci, k4 + 1)
                pe.wait_ge(w_rdy, k4 + 1)
                o = banks[:, 5 + g % 3, 0:w]
                pe.matmul(o, tri_sb[:, 0, :], ci_buf[g % RING][:, 0:w], start=True, stop=False)
                later = ci_buf[(g - 1) % RING] if i else ci_zero
                pe.matmul(o, tri_sb[:, 1, :], later[:, 0:w], start=False, stop=True).then_inc(c_done, 1)

            def neighbours(n, c, i):
                w = CHUNKS[c][1] * P
                k4 = n * NB + i
                pe.wait_ge(w_rdy, k4 + 5)
                if i == 0:
                    pe.wait_ge(c5, n + 1)
                b = 2 * (c % 2)
                for t in range(2):
                    j = NB - 1 - (i + t)
                    pe.matmul(banks[:, b, 0:w], spl[:, j, 0:2 * D], wt[(c * NB + i + t) % RING][:, 0:w],
                              start=(i + t == 0), stop=(i + t == NB - 1))
                for t in range(2):
                    j = NB - 1 - (i + t)
                    pe.matmul(banks[t * D:(t + 1) * D, b + 1, 0:w], spl[:, j, 2 * D:3 * D],
                              wt[(c * NB + i + t) % RING][:, 0:w], start=(i == 0), stop=(i == NB - 2)).then_inc(w_used, 1)

            def out5(n, c):
                pe.wait_ge(c5, n + 3)
                pe.wait_ge(y5, n + 1)
                for i in range(CHUNKS[c][1]):
                    o = banks[:, 4, i * D:(i + 1) * D]
                    pe.matmul(o, oh[:, i * P:(i + 1) * P], const("lw2"), start=True, stop=False)
                    last = pe.matmul(o, ol[:, i * P:(i + 1) * P], const("lw2"), start=False, stop=True)
                last.then_inc(o5, 1)

            with pe.Fori(0, 2) as k:
                steps = [(c, i) for c in range(NC) for i in range(NB)]
                for c, i in steps[:2]:
                    counts(k * NC + c, c, i)
                pe.wait_ge(spl_rdy, 1)
                for g in range(0, len(steps), 2):
                    for c, i in steps[g + 2:g + 4]:
                        counts(k * NC + c, c, i)
                    c, i = steps[g]
                    if c and i == 6:
                        out5(k * NC + (c - 1), c - 1)
                    neighbours(k * NC + c, c, i)
                out5(k * NC + (NC - 1), NC - 1)

            pe.wait_ge(pm_t, 1)
            pe.transpose(banks[0:1, 2, 0:P], cols[:, 0:1], ident).then_inc(pm_r, 1)
            pe.wait_ge(pm_t, 2)
            pe.matmul(banks[:, 3, 0:1], agg_flat[0:1, 0:P], cols[0:1, 2:3], start=True, stop=True).then_inc(fl_b, 1)
            pe.wait_ge(fl_i, 1)
            fast = pe.value_load(flag_i[0:1, 0:1], min_val=0, max_val=1)

            def aggregate(t, cnt, jb, s, counter):
                pe.matmul(banks[0:D + 1, t % 2, 0:cnt * P], nf[:, jb, :], s[:, 0:cnt * P],
                          start=(jb == 0), stop=(jb == NB - 1)).then_inc(s_used, 1)

            def back6(t, cnt):
                pe.wait_ge(e6, t + 3)
                for i in range(cnt):
                    last = pe.matmul(banks[:, 2, i * (D + 1):(i + 1) * (D + 1)], ot[:, i * P:(i + 1) * P],
                                     const("ident", D + 1)[:, 0:D + 1], start=True, stop=True)
                last.then_inc(b6, 1)

            def turn6(t, cnt):
                pe.wait_ge(z6, t + 1)
                for i in range(cnt // 2):
                    last = pe.transpose(banks[:, 3, i * P:(i + 1) * P], agg_flat[:, i * P:(i + 1) * P], ident)
                last.then_inc(t6, 1)

            def out6(t, cnt):
                pe.wait_ge(c6, t + 1)
                for i in range(cnt):
                    r, h = (i % 2) * D, i // 2
                    a, b = COLS["lw3"]
                    last = pe.matmul(out6_ps(i % 2, 2)[:, h, :], aggt[r:r + D, h * P:(h + 1) * P], cst[r:r + D, a:b],
                                     start=True, stop=True)
                last.then_inc(o6, 1)

            def forms(t, cnt, jb):
                pe.wait_ge(t_rdy, t * NB + (jb + (3 if jb < 2 else 1)))
                w = cnt * P
                o = banks[:, 4 + jb % RING, 0:w]
                for u, v, last in ((ua, va, False), (ub, vb, True)):
                    mv = v[:, t * STEP6 * P:t * STEP6 * P + w] if isinstance(t, int) else \
                        v[:, 0:FULL6 * STEP6 * P].rearrange("p (t w) -> p t w", t=FULL6)[:, t, :]
                    ins = pe.matmul(o, u[:, jb * P:(jb + 1) * P], mv, start=not last, stop=last)
                ins.then_inc(g_done, 1)

            def near(t, cnt, first, nxt):
                for jb in range(NB):
                    if jb + 2 < NB:
                        forms(t, cnt, jb + 2)
                    elif nxt:
                        forms(t + 1, nxt, jb + 2 - NB)
                    if not first:
                        if jb == 4:
                            back6(t - 1, STEP6)
                        if jb == 12:
                            turn6(t - 1, STEP6)
                        if jb == 16:
                            out6(t - 1, STEP6)
                    if jb % 2:
                        pe.wait_ge(sd_rdy, t * PAIRS + (jb // 2 + 1))
                    else:
                        pe.wait_ge(sp_rdy, t * PAIRS + (jb // 2 + 1))
                    if jb == 0:
                        pe.wait_ge(e6, t + 1)
                    aggregate(t, cnt, jb, st[jb % RING], None)

            with pe.If(fast != 0):
                pe.wait_ge(nat, 1)
                turned = 0
                for src, off, k in ((nu, 0, KA), (nu, KA, KB), (nv, 0, KA), (nv, KA, KB)):
                    for b0 in range(0, NB, 8):
                        pe.wait_ge(ft_c, turned + 1)
                        for b in range(b0, min(b0 + 8, NB)):
                            last = pe.transpose(banks[0:k, 4 + turned % RING, :].bitcast(BF16)[:, (b - b0) * P:(b - b0 + 1) * P],
                                                src[:, b, off:off + k], tri_sb[:, 2, :])
                        last.then_inc(ft_t, 1)
                        turned += 1
                pe.wait_ge(ft_c, RING + turned)
                for jb in range(2):
                    forms(0, STEP6, jb)
                over_chunks(pe, near)
            with pe.Else():
                turned = 0
                for rnd in range(3):
                    pe.wait_ge(nat, rnd + 1)
                    for b0 in range(0, NB, 4):
                        pe.wait_ge(ft_c, turned + 1)
                        for b in range(b0, min(b0 + 4, NB)):
                            last = pe.transpose(banks[0:NF, 4 + turned % RING, (b - b0) * P:(b - b0 + 1) * P],
                                                gu[:, b, :], ident)
                        last.then_inc(ft_t, 1)
                        turned += 1
                pe.wait_ge(ft_c, RING + turned)

                def general(t, cnt, first, nxt):
                    for jb in range(NB):
                        w = cnt * P
                        pe.wait_ge(t_rdy, t * NB + (jb + RING))
                        for b, v in ((4, vt), (5, vt2)):
                            mv = v[:, t * STEP6 * P:t * STEP6 * P + w] if isinstance(t, int) else \
                                v[:, 0:FULL6 * STEP6 * P].rearrange("p (t w) -> p t w", t=FULL6)[:, t, :]
                            ins = pe.matmul(banks[:, b, 0:w], ut[:, jb * P:(jb + 1) * P], mv, start=True, stop=True)
                        ins.then_inc(g_done, 1)
                        if not first:
                            if jb == 4:
                                back6(t - 1, STEP6)
                            if jb == 12:
                                turn6(t - 1, STEP6)
                            if jb == 16:
                                out6(t - 1, STEP6)
                        pe.wait_ge(t_rdy, t * NB + (jb + RING + 1))
                        if jb == 0:
                            pe.wait_ge(e6, t + 1)
                        aggregate(t, cnt, jb, gen_s, None)

                over_chunks(pe, general)
            back6(FULL6, REST6)
            turn6(FULL6, REST6)
            out6(FULL6, REST6)

        @block.scalar
        def _(act):
            for b in range(0, NB, 2):
                act.wait_ge(u_ps, b + 1)
                act.wait_ge(u_sb, b + 1)
                act.copy(u_all[:, :, b, :], banks[:, b % RING, 0:4 * D].rearrange("p (u c) -> p u c", u=4)).then_inc(u_sb, 1)

            def to_sbuf(n, c):
                w = CHUNKS[c][1] * P
                act.wait_ge(prod, n + 1)
                act.wait_ge(bk, n + 1)
                act.copy(yt[c % 2][:, 0:w], banks[:, c % 2, 0:w]).then_inc(y_rdy, 1)

            def early_half(src, h):
                act.copy(moving_h[:, h, :], halves(src)[:, h, :]).then_inc(m_ready, 1)

            def root(nb):
                act.activation(small[:, 3, 0:nb], small[:, 2, 0:nb], ACT.Sqrt).then_inc(rt, 1)

            act.wait_ge(m_ready, 2)
            for p, src in ((0, XW2), (1, XW1)):
                with act.Fori(0, 2) as k:
                    for c in range(NC):
                        to_sbuf(p * 2 * NC + k * NC + c, c)
                act.wait_ge(prod, 2 * NC * (p + 1))
                act.wait_ge(freed, 2 + 2 * NC * p + NC)
                early_half(src, 1 - p)
            with act.Fori(0, 2) as k:
                for c in range(NC):
                    to_sbuf(k * NC + (4 * NC + c), c)
                act.wait_ge(ve, k + 1)
                root(HB)
            act.wait_ge(ln_c, LN_STEPS)
            early_half(X1, 1)

            def turned4(m, c):
                w = CHUNKS[c][1] * P
                act.wait_ge(t4, m + 1)
                act.wait_ge(bk, m + (6 * NC + 2))
                act.copy(zxt[:, 0:w], banks[:, 4, 0:w]).then_inc(c4, 1)

            def tanh4(m, c):
                w = CHUNKS[c][1] * P
                act.wait_ge(h4, m + 1)
                act.activation(ht[:, 0:w], banks[:, 5, 0:w], ACT.Tanh, bias=hbias).then_inc(a4, 1)

            with act.Fori(0, 2) as k:
                for c in range(NC):
                    turned4(k * NC + c, c)
                    tanh4(k * NC + c, c)
                    to_sbuf(k * NC + (6 * NC + c), c)
                act.wait_ge(ve, k + 3)
                root(HB)

            def weights(n, c, i):
                k4 = n * NB + i
                g = c * NB + i
                w = CHUNKS[c][1] * P
                act.wait_ge(c_done, k4 + 4)
                act.wait_ge(w_used, k4 + 1)
                act.activation(wt[g % RING].bitcast(U16)[:, 0:w], banks[:, 5 + g % 3, 0:w], ACT.Relu,
                               bias=cols[:, 11:12]).then_inc(w_rdy, 1)

            def sums5(n, c):
                w = CHUNKS[c][1] * P
                act.wait_ge(w_used, n * NB + (RING + NB))
                act.wait_ge(o5, n + 1)
                act.mul(oh[:, 0:w], banks[:, 2 * (c % 2), 0:w], UNSCALE)
                act.mul(ol[:, 0:w], banks[:, 2 * (c % 2) + 1, 0:w], UNSCALE).then_inc(c5, 1)

            with act.Fori(0, 2) as k:
                for c in range(NC):
                    for i in range(NB):
                        weights(k * NC + c, c, i)
                        if c and i == 3:
                            sums5(k * NC + (c - 1), c - 1)
                sums5(k * NC + (NC - 1), NC - 1)
            act.wait_ge(ve, 5)
            root(NB)

            act.wait_ge(fl_i, 1)
            fast = act.value_load(flag_i[0:1, 0:1], min_val=0, max_val=1)

            def sums6(t, cnt):
                act.wait_ge(s_used, t * NB + (RING + NB))
                act.wait_ge(b6, t + 1)
                act.copy(ot[:, 0:cnt * P], banks[0:D + 1, t % 2, 0:cnt * P]).then_inc(e6, 1)

            def turned6(t, cnt):
                act.wait_ge(t6, t + 1)
                act.copy(aggt[:, 0:cnt // 2 * P], banks[:, 3, 0:cnt // 2 * P]).then_inc(c6, 1)

            def squares(t, cnt, first, nxt):
                for jb in range(NB):
                    w = cnt * P
                    act.wait_ge(g_done, t * NB + (jb + 1))
                    act.wait_ge(t_rdy, t * NB + (jb + RING - 1))
                    act.activation(sq[jb % 2][:, 0:w], banks[:, 4 + jb % RING, 0:w], ACT.Square,
                                   bias=cols[:, 10:11]).then_inc(q_done, 1)
                    if not first and jb == 4:
                        sums6(t - 1, STEP6)
                    if not first and jb == 13:
                        turned6(t - 1, STEP6)

            with act.If(fast != 0):
                turned = 0
                for dst, k in ((ua, KA), (ub, KB), (va, KA), (vb, KB)):
                    for b0 in range(0, NB, 8):
                        if turned % 2 == 0:
                            w = min(8, NB - b0) * P
                            act.wait_ge(ft_t, turned + 1)
                            act.wait_ge(ft_c, turned + RING)
                            act.copy(dst[:, b0 * P:b0 * P + w], banks[0:k, 4 + turned % RING, :].bitcast(BF16)[:, 0:w])\
                                .then_inc(ft_c, 1)
                        turned += 1
                over_chunks(act, squares)
            with act.Else():
                turned = 0
                for dst in (ut, vt, vt2):
                    for b0 in range(0, NB, 4):
                        w = min(4, NB - b0) * P
                        act.wait_ge(ft_t, turned + 1)
                        act.copy(dst[:, b0 * P:b0 * P + w], banks[0:NF, 4 + turned % RING, 0:w]).then_inc(ft_c, 1)
                        turned += 1

                def general(t, cnt, first, nxt):
                    with act.Fori(0, NB) as jb:
                        w = cnt * P
                        it = t * NB + jb
                        act.wait_ge(gv, 2 * it + 1)
                        act.activation(gen[3][:, 0:w], gen[2][:, 0:w], ACT.Sqrt).then_inc(ga, 1)
                        act.wait_ge(gv, 2 * it + 2)
                        act.activation(gen[5][:, 0:w], gen[4][:, 0:w], ACT.Ln, bias=1.0, scale=1.0)
                        act.activation(gen[6][:, 0:w], gen[4][:, 0:w], ACT.Ln, bias=1.0, scale=-1.0).then_inc(ga, 1)
                        if not first:
                            with act.If(jb == 4):
                                sums6(t - 1, STEP6)
                            with act.Else():
                                act.wait_ge(fl_i, 1)
                            with act.If(jb == 13):
                                turned6(t - 1, STEP6)
                            with act.Else():
                                act.wait_ge(fl_i, 1)

                over_chunks(act, general)
            sums6(FULL6, REST6)
            turned6(FULL6, REST6)
            act.wait_ge(vr, 1)
            act.activation(small[:, 1, :], small[:, 0, :], ACT.Sqrt).then_inc(th, 1)
            act.wait_ge(vr, 2)
            act.activation(small[:, 5, :], small[:, 4, :], ACT.Tanh).then_inc(th, 1)
            act.wait_ge(ve, 6)
            root(NB)

        @block.vector
        def _(dve):
            linked = [0]

            def chain(ins):
                linked[0] += 1
                ins.then_inc(link, 1)
                dve.wait_ge(link, linked[0])

            for s, n in ((u_sb, 1), (y_rdy, 2), (bk, 2), (freed, 2), (c4, 1), (a4, 1), (y4, 2), (c_done, 3), (w_rdy, 3),
                         (w_used, RING), (c5, 2), (o5, 1), (y5, 1), (ft_c, RING), (t_rdy, RING), (s_used, RING),
                         (e6, 2), (b6, 1), (rs_ps, RS_RING)):
                dve.sem_inc(s, n)
            chain(dve.memset(cols[:, 11:12], MASK_BIAS))
            chain(dve.memset(cols[:, 10:11], ROOT - MID))
            dve.wait_ge(c_ld, 32)
            chain(dve.tensor_scalar(hbias, const("w1t"), const("tcol"), const("b1"), ALU.mult, ALU.add))
            for b in range(1, NB, 2):
                dve.wait_ge(u_ps, b + 1)
                dve.wait_ge(u_sb, b + 1)
                dve.tensor_copy(u_all[:, :, b, :], banks[:, b % RING, 0:4 * D].rearrange("p (u c) -> p u c", u=4)).then_inc(u_sb, 1)
            dve.wait_ge(u_sb, NB + 1)
            dve.tensor_tensor(region(XW1), region(XW1), region(XW3), ALU.subtract)
            dve.tensor_scalar(words(0, REGION), region(XW3), 2.0, None, ALU.mult).then_inc(m_ready, 2)
            chain(dve.tensor_scalar(region(XW2), region(XW2), 2.0, None, ALU.mult))
            dve.wait_ge(m_ready, 2)

            def natural(c):
                return banks[:, 2 + c % 2, 0:CHUNKS[c][1] * D]

            def pass0(n, k, c):
                dve.wait_ge(bk, n + 3)
                o = rows(XW2, (k + 1) % 2, *CHUNKS[c])
                dve.scalar_tensor_tensor(o, natural(c), 2.0, o, ALU.mult, ALU.add).then_inc(freed, 1)

            with dve.Fori(0, 2) as k:
                for c, (s0, cnt) in enumerate(CHUNKS):
                    for s in range(s0, s0 + cnt):
                        dve.wait_ge(arrived, k * HB + (s + 1))
                        dve.wait_ge(rs_ps, k * HB + (s + 1 + (RS_RING - rs_gap(s))))
                        dve.tensor_reduce(rsp[:, rs_buf(s), :], a_slot[:, s, :, :].rearrange("p j i -> p i j"), AX_X, ALU.add)\
                            .then_inc(rs_sum, 1)
                    if c:
                        pass0(k * NC + (c - 1), k, c - 1)
                pass0(k * NC + (NC - 1), k, NC - 1)
                dve.wait_ge(rs_ps, k * HB + (HB + RS_RING))
                h = (k + 1) % 2
                dve.tensor_scalar(neg_rs[:, :].rearrange("p (h s) -> p h s", h=2)[:, h, :], banks[:, 4, 0:HB], -1.0, None, ALU.mult)
            dve.wait_ge(prod, 2 * NC)
            dve.wait_ge(freed, 2 + 2 * NC)
            dve.tensor_copy(moving_h[:, 0, :], halves(XW2)[:, 0, :]).then_inc(m_ready, 1)
            chain(dve.scalar_tensor_tensor(region(XW0), region(XW2), -0.5, region(XW0), ALU.mult, ALU.add))

            with dve.Fori(0, 2) as k:
                for c in range(NC):
                    dve.wait_ge(bk, k * NC + (2 * NC + c + 3))
                    o = rows(XW1, k, *CHUNKS[c])
                    dve.tensor_tensor(o, natural(c), o, ALU.add).then_inc(freed, 1)
            dve.wait_ge(prod, 4 * NC)
            dve.wait_ge(freed, 2 + 4 * NC)
            dve.tensor_copy(moving_h[:, 1, :], halves(XW1)[:, 1, :]).then_inc(m_ready, 1)

            def norm(y, x, base, nb, roots):
                n = [0]

                def step(ins):
                    n[0] += 1
                    ins.then_inc(ln_c, 1)
                    dve.wait_ge(ln_c, base + n[0])

                def col(i):
                    return stats[:, 0:nb, i]

                mean, dif, var, std, rec = (small[:, i, 0:nb] for i in (0, 1, 2, 3, 4))
                dve.tensor_tensor(mean, col(1), col(4), ALU.add)
                dve.tensor_tensor(dif, col(1), col(4), ALU.subtract)
                step(dve.tensor_tensor(var, col(2), col(5), ALU.add))
                step(dve.tensor_scalar(mean, mean, 0.5, None, ALU.mult))
                step(dve.tensor_tensor(dif, dif, dif, ALU.mult))
                step(dve.scalar_tensor_tensor(var, dif, D / 4.0, var, ALU.mult, ALU.add))
                step(dve.tensor_scalar(var, var, 0.25 / D, EPS / 4, ALU.mult, ALU.add))
                dve.sem_inc(ve, 1)
                step(dve.tensor_tensor(x, y, mean.unsqueeze(2).to_broadcast([P, nb, D]), ALU.subtract))
                dve.wait_ge(rt, roots + 1)
                step(dve.reciprocal(rec, std))
                step(dve.tensor_tensor(rec, rec, var, ALU.mult))
                step(dve.tensor_tensor(std, std, rec, ALU.add))
                step(dve.reciprocal(rec, std))
                step(dve.tensor_tensor(x, x, rec.unsqueeze(2).to_broadcast([P, nb, D]), ALU.mult))
                assert n[0] == LN_STEPS

            def stats_of(ap, s0, cnt):
                for s in range(s0, s0 + cnt):
                    last = dve.bn_stats(stats[:, s, :], ap[:, (s - s0) * D:(s - s0 + 1) * D])
                return last

            def by_block(ap):
                return ap.rearrange("p (s c) -> p s c", c=D)

            with dve.Fori(0, 2) as k:
                h = (k + 1) % 2
                for c in range(NC + 1):
                    n = k * NC + (4 * NC + c)
                    dve.wait_ge(freed, n + 2)
                    if c < NC:
                        dve.wait_ge(bk, n + 3)
                        o = rows(XW0, h, *CHUNKS[c])
                        dve.tensor_tensor(o, natural(c), o, ALU.add).then_inc(freed, 1)
                    else:
                        dve.tensor_copy(cols[:, 8:9], hbias)
                    if c:
                        last = stats_of(rows(XW0, h, *CHUNKS[c - 1]), *CHUNKS[c - 1])
                last.then_inc(link, 1)
                dve.wait_ge(link, k + (linked[0] + 1))
                norm(by_block(halves(XW0)[:, h, :]), by_block(halves(X1)[:, h, :]), k * LN_STEPS, HB, k)
            linked[0] += 2
            dve.wait_ge(prod, 6 * NC)
            dve.tensor_copy(moving_h[:, 0, :], halves(X1)[:, 0, :]).then_inc(m_ready, 1)
            dve.wait_ge(m_ready, 8)

            def features4(k, c):
                s0, cnt = CHUNKS[c]
                m = k * NC + c
                dve.wait_ge(c4, m + 1)
                x = moving_h[:, k, s0 * D:(s0 + cnt) * D].rearrange("p (s c) -> p s c", c=D)
                rs = neg_rs[:, :].rearrange("p (h s) -> p h s", h=2)[:, k, s0:s0 + cnt]
                dve.tensor_copy(zx[:, 0:cnt, D:2 * D], x)
                dve.tensor_tensor(zx[:, 0:cnt, 0:D], x, rs.unsqueeze(2).to_broadcast([P, cnt, D]), ALU.mult)\
                    .then_inc(zx_r, 1)

            def read4(k, c):
                s0, cnt = CHUNKS[c]
                m = k * NC + c
                dve.wait_ge(bk, m + (6 * NC + 3))
                dve.tensor_tensor(by_block(rows(Y1, k, s0, cnt)), banks[:, 6 + c % 2, 0:cnt * D].rearrange("p (s c) -> p s c", c=D),
                                  const("b2").unsqueeze(1).to_broadcast([P, cnt, D]), ALU.add).then_inc(y4, 1)

            with dve.Fori(0, 2) as k:
                for c in range(NC):
                    features4(k, c)
                    if c:
                        read4(k, c - 1)
                read4(k, NC - 1)
                dve.wait_ge(y4, k * NC + (NC + 2))
                dve.tensor_copy(cols[:, 8:9], hbias)
                last = stats_of(halves(Y1)[:, k, :], 0, HB)
                last.then_inc(link, 1)
                dve.wait_ge(link, k + (linked[0] + 1))
                norm(by_block(halves(Y1)[:, k, :]), by_block(halves(X2)[:, k, :]), k * LN_STEPS + 2 * LN_STEPS, HB, k + 2)
            linked[0] += 2
            x2, rest = blocks(X2), blocks(Y1)
            chain(dve.tensor_copy(spl[:, :, 0:D], x2))
            chain(dve.tensor_tensor(rest, x2, spl[:, :, 0:D], ALU.subtract))
            chain(dve.tensor_copy(spl[:, :, D:2 * D], rest))
            dve.tensor_tensor(spl[:, :, 2 * D:3 * D], rest, spl[:, :, D:2 * D], ALU.subtract).then_inc(spl_rdy, 1)
            dve.wait_ge(spl_rdy, 1)
            chain(dve.memset(ci_zero, 0.0))
            chain(dve.tensor_tensor(x2, x2, const("lb2").unsqueeze(1).to_broadcast([P, NB, D]), ALU.add))

            def masks(k, n, c, i):
                k4 = n * NB + i
                g = c * NB + i
                s0, cnt = CHUNKS[c]
                dve.wait_ge(c_done, k4 + 1)
                if i == 0:
                    dve.wait_ge(arrived, k * HB + (4 * HB + s0 + cnt))
                else:
                    dve.wait_ge(ci, k4)
                later = ci_buf[(g - 1) % RING] if i else ci_zero
                dve.scalar_tensor_tensor(split(ci_buf[g % RING], cnt), a_slot[:, s0:s0 + cnt, NB - 1 - i, :], 0.0,
                                         split(later, cnt), ALU.not_equal, ALU.add).then_inc(ci, 1)

            def read5(k, c):
                s0, cnt = CHUNKS[c]
                dve.wait_ge(o5, k * NC + (c + 2))
                o = rows(X2, (k + 1) % 2, s0, cnt)
                dve.tensor_tensor(o, banks[:, 4, 0:cnt * D], o, ALU.add).then_inc(y5, 1)

            with dve.Fori(0, 2) as k:
                for c in range(NC):
                    for i in range(NB):
                        masks(k, k * NC + c, c, i)
                        if c and i == 12:
                            read5(k, c - 1)
                read5(k, NC - 1)
            dve.wait_ge(y5, 1 + 2 * NC)
            chain(stats_of(region(X2), 0, NB))
            norm(x2, x3, 4 * LN_STEPS, NB, 4)

            nrm, bb, dev, mm, deg, beta, g1, bg1 = (small[:, i, :] for i in range(8))
            chain(dve.memset(agg_flat[0:1, 0:P], 1.0))
            chain(dve.tensor_tensor(v3, x3, x3, ALU.mult))
            chain(dve.tensor_reduce(nrm, v3, AX_X, ALU.add))
            dve.tensor_scalar(bb, nrm, -1.0, 1.0, ALU.mult, ALU.add)
            chain(dve.tensor_scalar(dev, nrm, -float(D), None, ALU.add))
            chain(dve.scalar_tensor_tensor(dev, dev, -1.0, dev, ALU.mult, ALU.max))
            chain(dve.tensor_tensor(dev[:, NB - 1:NB], dev[:, NB - 1:NB], const("valid"), ALU.mult))
            dve.tensor_reduce(cols[:, 0:1], dev, AX_X, ALU.max).then_inc(pm_t, 1)
            dve.tensor_scalar(mm, bb, MIN_NORM, None, ALU.max)
            chain(dve.tensor_scalar(deg, neg_rs[:, :], -1.0, 1e-8, ALU.mult, ALU.max))
            chain(dve.reciprocal(deg, deg))
            chain(dve.tensor_tensor(g1, mm, deg, ALU.mult))
            dve.wait_ge(pm_r, 1)
            chain(dve.tensor_reduce(cols[0:1, 1:2], banks[0:1, 2, 0:P], AX_X, ALU.max))
            dve.tensor_scalar(cols[0:1, 2:3], cols[0:1, 1:2], NEAR, None, ALU.is_le).then_inc(pm_t, 1)
            dve.wait_ge(pm_t, 2)
            chain(dve.tensor_copy(flag_i[:, :], cols[0:1, 2:3]))
            dve.sem_inc(fl_i, 1)
            dve.wait_ge(fl_b, 1)
            flag = cols[:, 3:4]
            chain(dve.tensor_copy(flag, banks[:, 3, 0:1]))
            dve.tensor_scalar(cols[:, 4:5], flag, C3 - 1.0, 1.0, ALU.mult, ALU.add)
            chain(dve.tensor_scalar(beta, bb, -1.0, flag, ALU.add, ALU.mult))
            chain(dve.tensor_scalar(beta, beta, 1.0, None, ALU.add))
            chain(dve.reciprocal(beta, beta))
            nb_ = dev
            dve.tensor_tensor(nf[:, :, 0:D], x3, beta.unsqueeze(2).to_broadcast([P, NB, D]), ALU.mult)
            chain(dve.tensor_tensor(nb_, nrm, beta, ALU.mult))
            chain(dve.tensor_tensor(nf[:, :, D], nb_, beta, ALU.add))
            fast = dve.value_load(flag_i[0:1, 0:1], min_val=0, max_val=1)

            def factors():
                chain(dve.tensor_tensor(g1, g1, beta, ALU.mult))
                chain(dve.tensor_scalar(g1, g1, cols[:, 4:5], None, ALU.mult))
                chain(dve.tensor_tensor(bg1, bb, g1, ALU.mult))

            def some(t, cnt, ap, width):
                if isinstance(t, int):
                    return ap[:, t * STEP6 * width:(t * STEP6 + cnt) * width]
                return ap[:, 0:FULL6 * STEP6 * width].rearrange("p (t w) -> p t w", t=FULL6)[:, t, :]

            GATHER = 7

            def gather6(t, cnt):
                n = [0]

                def step(ins):
                    n[0] += 1
                    ins.then_inc(gl, 1)
                    dve.wait_ge(gl, t * GATHER + n[0])

                x = by_block(some(t, cnt, region(X2), D))
                o = banks[:, 2, 0:cnt * (D + 1)].rearrange("p (b c) -> p b c", c=D + 1)
                tmp, e = tmp6[:, 0:cnt, :], cols[:, 4:4 + cnt]
                dve.wait_ge(b6, t + 2)
                step(dve.tensor_tensor(tmp, o[:, :, 0:D], x, ALU.mult))
                step(dve.tensor_reduce(e, tmp, AX_X, ALU.add))
                step(dve.scalar_tensor_tensor(e, e, -2.0, o[:, :, D], ALU.mult, ALU.add))
                step(dve.tensor_tensor(e, e, some(t, cnt, g1, 1), ALU.mult))
                step(dve.tensor_tensor(tmp, x, e.unsqueeze(2).to_broadcast([P, cnt, D]), ALU.mult))
                step(dve.tensor_tensor(agg[:, 0:cnt, :], o[:, :, 0:D],
                                       some(t, cnt, bg1, 1).unsqueeze(2).to_broadcast([P, cnt, D]), ALU.mult))
                step(dve.tensor_tensor(agg[:, 0:cnt, :], agg[:, 0:cnt, :], tmp, ALU.subtract))
                dve.sem_inc(z6, 1)
                assert n[0] == GATHER

            def read6(t, cnt):
                dve.wait_ge(o6, t + 1)
                o = some(t, cnt, words(NB * (D + 1), REGION), D).rearrange("p (b u c) -> p u b c", u=2, c=D)
                for odd in range(2):
                    last = dve.tensor_tensor(o[:, odd], out6_ps(odd, cnt // 2),
                                             const("lb3").unsqueeze(1).to_broadcast([P, cnt // 2, D]), ALU.add)
                last.then_inc(y6, 1)

            def near(t, cnt, first, nxt):
                for jb in range(NB):
                    w = cnt * P
                    dve.wait_ge(q_done, t * NB + (jb + 1))
                    dve.wait_ge(s_used, t * NB + (jb + (3 if jb < 2 else 1)))
                    dve.scalar_tensor_tensor(st[jb % RING][:, 0:w], sq[jb % 2][:, 0:w], FAR,
                                             banks[:, 4 + jb % RING, 0:w], ALU.add, ALU.mult).then_inc(t_rdy, 1)
                    if jb % 2:
                        s = split(st[jb % RING], cnt)
                        dve.wait_ge(arrived, t + (6 * HB - 1))
                        dve.wait_ge(t_rdy, t * NB + (RING + jb + 1))
                        dve.tensor_tensor(s, s, a6(t, jb, cnt), ALU.mult).then_inc(sd_rdy, 1)
                    if not first:
                        if jb == 3:
                            dve.wait_ge(sd_rdy, t * PAIRS)
                            dve.wait_ge(sp_rdy, t * PAIRS)
                            dve.sem_inc(a_used, 1)
                        if jb == 8:
                            gather6(t - 1, STEP6)
                        if jb == 20:
                            read6(t - 1, STEP6)

            with dve.If(fast != 0):
                saved = linked[0]
                xb = nf[:, :, 0:D]
                chain(dve.tensor_copy(nu[:, :, 0:D], xb))
                dve.tensor_copy(nu[:, :, D:2 * D], nu[:, :, 0:D])
                chain(dve.tensor_tensor(nu[:, :, KA:KA + D], xb, nu[:, :, 0:D], ALU.subtract))
                dve.tensor_scalar(nv[:, :, 0:D], nu[:, :, 0:D], -2.0, None, ALU.mult)
                dve.tensor_scalar(nv[:, :, D:2 * D], nu[:, :, KA:KA + D], -2.0, None, ALU.mult)
                dve.tensor_scalar(nv[:, :, KA:KA + D], nu[:, :, 0:D], -2.0, None, ALU.mult)
                r = tmp6.rearrange("p b c -> p (b c)")[:, 0:NB]
                for at_, src in ((0, nb_), (3, beta)):
                    chain(dve.tensor_copy(parts[:, :, at_], src))
                    chain(dve.tensor_tensor(r, src, parts[:, :, at_], ALU.subtract))
                    chain(dve.tensor_copy(parts[:, :, at_ + 1], r))
                    chain(dve.tensor_tensor(parts[:, :, at_ + 2], r, parts[:, :, at_ + 1], ALU.subtract))
                chain(dve.tensor_copy(parts[:, :, 6:9], parts[:, :, 0:3]))
                ex = KA + D
                for i, (a, b) in enumerate(((0, 0), (0, 1), (1, 0), (1, 1), (0, 2), (2, 0))):
                    dve.tensor_copy(nu[:, :, ex + i:ex + i + 7:6], parts[:, :, a:a + 4:3])
                    dve.tensor_copy(nv[:, :, ex + i:ex + i + 7:6], parts[:, :, 3 + b:3 + b + 4:3])
                dve.memset(nu[:, :, ex + 12:ex + 15], 1.0)
                dve.memset(nu[:, :, ex + 15:ex + 16], 0.0)
                for i, part in enumerate(ROOT_PARTS):
                    dve.memset(nv[:, :, ex + 12 + i:ex + 13 + i], -part)
                dve.memset(nv[:, :, ex + 15:ex + 16], 0.0).then_inc(nat, 1)
                factors()
                turned = 0
                for dst, k in ((ua, KA), (ub, KB), (va, KA), (vb, KB)):
                    for b0 in range(0, NB, 8):
                        if turned % 2 == 1:
                            w = min(8, NB - b0) * P
                            dve.wait_ge(ft_t, turned + 1)
                            dve.wait_ge(ft_c, turned + RING)
                            dve.tensor_copy(dst[:, b0 * P:b0 * P + w], banks[0:k, 4 + turned % RING, :].bitcast(BF16)[:, 0:w])\
                                .then_inc(ft_c, 1)
                        turned += 1
                over_chunks(dve, near)
                linked[0], saved = saved, linked[0]
            with dve.Else():
                NT = (NB + 3) // 4
                chain(dve.memset(gu[:, :, D + 1:D + 3], 1.0))
                chain(dve.tensor_copy(gu[:, :, 0:D], x3))
                dve.tensor_copy(gu[:, :, D], nrm).then_inc(nat, 1)
                dve.wait_ge(ft_c, RING + NT)
                chain(dve.memset(gu[:, :, D + 2:D + 3], 0.0))
                chain(dve.memset(gu[:, :, D:D + 1], 1.0))
                dve.tensor_scalar(gu[:, :, 0:D], x3, -2.0, None, ALU.mult)
                dve.tensor_copy(gu[:, :, D + 1], nrm).then_inc(nat, 1)
                dve.wait_ge(ft_c, RING + 2 * NT)
                chain(dve.memset(gu[:, :, D + 1:D + 2], 1.0))
                dve.tensor_copy(gu[:, :, D], nrm).then_inc(nat, 1)
                factors()
                KG = 26

                def general(t, cnt, first, nxt):
                    w = cnt * P
                    with dve.Fori(0, NB) as jb:
                        it = t * NB + jb
                        n = [0]

                        def step(ins):
                            n[0] += 1
                            ins.then_inc(gc, 1)
                            dve.wait_ge(gc, it * KG + n[0])

                        dm, rec, r, root, z, lp, lm, f, qq, mask, tmp = (g[:, 0:w] for g in gen[0:11])
                        den, d2 = banks[:, 5, 0:w], banks[:, 4, 0:w]
                        dve.wait_ge(g_done, it + 1)
                        step(dve.tensor_scalar(dm, den, MIN_NORM, None, ALU.max))
                        step(dve.reciprocal(rec, dm))
                        step(dve.scalar_tensor_tensor(r, d2, 0.0, rec, ALU.max, ALU.mult))
                        step(dve.tensor_scalar(r, r, MIN_NORM * MIN_NORM, None, ALU.max))
                        dve.sem_inc(gv, 1)
                        dve.wait_ge(ga, 2 * it + 1)
                        step(dve.tensor_scalar(z, root, TANH_CLIP, None, ALU.min))
                        dve.sem_inc(gv, 1)
                        step(dve.tensor_scalar(qq, r, SMALL, None, ALU.min))
                        step(dve.tensor_scalar(mask, r, SMALL, None, ALU.is_gt))
                        step(dve.tensor_scalar(f, qq, 1 / 13, SERIES[0], ALU.mult, ALU.add))
                        for coef in SERIES[1:]:
                            step(dve.tensor_tensor(f, f, qq, ALU.mult))
                            step(dve.tensor_scalar(f, f, coef, None, ALU.add))
                        step(dve.reciprocal(tmp, root))
                        dve.wait_ge(ga, 2 * it + 2)
                        step(dve.tensor_tensor(lp, lp, lm, ALU.subtract))
                        step(dve.scalar_tensor_tensor(lp, lp, 0.5, tmp, ALU.mult, ALU.mult))
                        step(dve.tensor_tensor(lp, lp, mask, ALU.mult))
                        step(dve.tensor_scalar(mask, mask, -1.0, 1.0, ALU.mult, ALU.add))
                        step(dve.tensor_tensor(f, f, mask, ALU.mult))
                        step(dve.tensor_tensor(f, f, lp, ALU.add))
                        step(dve.tensor_tensor(f, f, rec, ALU.mult))
                        assert n[0] == KG, n[0]
                        dve.wait_ge(arrived, t + (6 * HB - 1))
                        dve.wait_ge(s_used, it + RING)
                        by_j = slots[:, 0:SLOTS6 * SLOT].rearrange("p (t b j i) -> p j t b i", t=2, b=STEP6, j=NB)
                        dve.tensor_tensor(split(gen_s, cnt), split(f, cnt), by_j[:, jb, t % 2, 0:cnt, :], ALU.mult)\
                            .then_inc(t_rdy, 1)
                        if not first:
                            with dve.If(jb == 8):
                                dve.sem_inc(a_used, 1)
                                gather6(t - 1, STEP6)
                            with dve.Else():
                                dve.wait_ge(fl_i, 1)
                            with dve.If(jb == 20):
                                read6(t - 1, STEP6)
                            with dve.Else():
                                dve.wait_ge(fl_i, 1)

                over_chunks(dve, general)
            gather6(FULL6, REST6)
            read6(FULL6, REST6)

            nf_ = [0]

            def fstep(ins):
                nf_[0] += 1
                ins.then_inc(fin, 1)
                dve.wait_ge(fin, nf_[0])

            dve.wait_ge(y6, FULL6 + 1)
            sqo = nf[:, :, 0:D]
            ss, root, rec, vn, tanh = (small[:, i, :] for i in (0, 1, 2, 4, 5))
            fstep(dve.tensor_tensor(sqo, v3, v3, ALU.mult))
            fstep(dve.tensor_reduce(ss, sqo, AX_X, ALU.add))
            dve.sem_inc(vr, 1)
            dve.wait_ge(th, 1)
            fstep(dve.tensor_scalar(root, root, MIN_NORM, None, ALU.max))
            fstep(dve.reciprocal(rec, root))
            fstep(dve.tensor_tensor(rec, rec, ss, ALU.mult))
            fstep(dve.tensor_tensor(vn, rec, root, ALU.add))
            fstep(dve.tensor_scalar(vn, vn, 0.5, MIN_NORM, ALU.mult, ALU.max))
            dve.sem_inc(vr, 1)
            fstep(dve.reciprocal(rec, vn))
            dve.wait_ge(th, 2)
            fstep(dve.tensor_tensor(rec, rec, tanh, ALU.mult))
            fstep(dve.tensor_tensor(v3, v3, rec.unsqueeze(2).to_broadcast([P, NB, D]), ALU.mult))
            fstep(dve.tensor_tensor(v3, v3, x3, ALU.add))
            fstep(stats_of(words(NB * (D + 1), REGION), 0, NB))
            norm(v3, v3, 5 * LN_STEPS, NB, 5)
            dve.sem_inc(fin, 1)
            assert nf_[0] + 1 == FIN_ALL


def kernel(**inputs):
    import numpy as np
    import ml_dtypes
    import concourse.bacc as _bacc
    from concourse import mybir as _mybir
    from concourse.bass_utils import run_bass_kernel_spmd as _run

    g = {k: np.ascontiguousarray(v) for k, v in inputs.items()}
    f32 = np.float32
    adj = np.zeros((NP, NP), f32)
    adj[:N, :N] = g["adj"]
    a_blocks = np.ascontiguousarray(adj.reshape(NB, P, NB, P).transpose(0, 3, 2, 1)).reshape(NB, P, NB * P)
    xt = np.zeros((D + 1, NP), f32)
    xt[:D, :N] = g["x"].T
    xt[D] = 1.0
    w = g["L0_gnn_weights"]
    wcat = np.zeros((D + 1, 4 * D), f32)
    for i, k in enumerate((3, 2, 1, 0)):
        wcat[:D, i * D:(i + 1) * D] = w[k]
    wcat[D, 3 * D:] = g["L0_gnn_bias"]
    consts = np.zeros((P, NCONST), f32)

    def put(name, a, row=0):
        consts[row:row + a.shape[0], COLS[name][0]:COLS[name][1]] = a

    put("ident", np.eye(P, dtype=f32))
    for half in (0, D):
        put("fold", np.eye(D, dtype=f32), half)
        put("bt", g["L1_gnn_B"].T, half)
        put("lw2", g["L2_gnn_weight"], half)
        put("lw3", g["L3_gnn_weight"], half)
    put("qb", g["L1_gnn_B"].T)
    put("qb", np.eye(D, dtype=f32), D)
    put("w1", g["L1_gnn_W1"][:D], D)
    put("w2", g["L1_gnn_W2"])
    for name, key in (("b2", "L1_gnn_b2"), ("lb2", "L2_gnn_bias"), ("lb3", "L3_gnn_bias")):
        put(name, np.repeat(g[key][None], P, 0))
    put("tcol", np.repeat(g["L1_gnn_t"][None], P, 0))
    put("w1t", g["L1_gnn_W1"][D][:, None])
    put("b1", g["L1_gnn_b1"][:, None])
    put("valid", (np.arange(P) < N - (NB - 1) * P).astype(f32)[:, None])
    put("one", np.ones((P, 1), f32))
    k, j = np.indices((P, P))
    t0 = np.where(k > j, -UNIT, 0) + np.where(k == j, UNIT * DIAG, 0)
    t1 = -UNIT - t0
    tri = np.stack([t0, t1, np.eye(P)], 1).astype(ml_dtypes.bfloat16)

    nc = _bacc.Bacc("TRN2", target_bir_lowering=False, num_devices=1)
    arrays = {"a_blocks": a_blocks, "xt": xt, "wcat": wcat, "consts": consts, "tri": tri}
    args = [nc.dram_tensor(n, a.shape, _mybir.dt.from_np(a.dtype), kind="ExternalInput").ap() for n, a in arrays.items()]
    args.append(nc.dram_tensor("out", (N, D), _mybir.dt.float32, kind="ExternalOutput").ap())
    gnn_kernel(nc, *args)
    r = _run(nc, [arrays], core_ids=[0])
    return r.results[0]["out"]
```

```python
import struct
from contextlib import ExitStack

import concourse.bass as bass
from concourse import mybir

F32 = mybir.dt.float32
BF16 = mybir.dt.bfloat16
U16 = mybir.dt.uint16
I32 = mybir.dt.int32
ALU = mybir.AluOpType
ACT = mybir.ActivationFunctionType
AX_X = mybir.AxisListType.X

P = 128
N = 3327
D = 64
NB = (N + P - 1) // P
NP = NB * P
HB = NB // 2
EPS = 1e-5

CHUNKS = [(0, 3), (3, 4), (7, 3), (10, 3)]
NC = len(CHUNKS)
PAIRS = NB // 2
assert sum(c for _, c in CHUNKS) == HB and NB % 2 == 0

CUT = 100
UNIT = 128
DIAG = 128
MASK_BIAS = float(UNIT * CUT - UNIT * DIAG)
UNSCALE = 2.0 ** 27

NEAR = 0.5
ROOT = 1.39459825
MID = -0.04442543
FAR = 1.32681359 ** 2
C3 = -0.40685946
TANH_CLIP = 1.0 - 1e-5
MIN_NORM = 1e-15
SMALL = 0.0625
SERIES = [1 / 11, 1 / 9, 1 / 7, 1 / 5, 1 / 3, 1.0]

COLS = {}
_at = 0
for _name, _w in (("ident", P), ("fold", D), ("bt", D), ("qb", D), ("w1", P), ("w2", D), ("lw2", D), ("lw3", 2 * D),
                  ("b2", D), ("lb2", D), ("lb3", D), ("tcol", 1), ("w1t", 1), ("b1", 1), ("valid", 1), ("one", 1), ("sel", 1)):
    COLS[_name] = (_at, _at + _w)
    _at += _w
NCONST = _at

SLOT = NB * P
STEP6 = 4
SLOTS6 = 8
FULL6 = NB // STEP6
REST6 = NB - FULL6 * STEP6
ON_POOL = [jb % 2 == 0 or jb in (7, 11, 15, 19) for jb in range(NB)]
NF = D + 3
KA, KB = 2 * D, D + 16
HALF_NAT = KB + D
RING = 4
QUARTER = P // 4
EARLY_CHUNK = FULL6 - 1
S_RING = HB
AHEAD6 = 6
LN_STEPS = 11
EARLY_NORMS = [(HB, NB, (1, 21), (2, 7)), (0, CHUNKS[2][0], (3, 3), (3, 8))]
LATE0 = CHUNKS[2][0]
FIN_STEPS = 13
EARLY = (FULL6 - 2) * STEP6
RS_RING = 6


def rs_buf(s):
    return s % RS_RING


def rs_gap(s):
    return RS_RING if s >= RS_RING else next(d for d in range(1, HB + 1) if (s - d) % HB % RS_RING == s)


def bf16_parts(v):
    parts = []
    for _ in range(3):
        u = struct.unpack("<I", struct.pack("<f", v))[0]
        u = (u + 0x7FFF + ((u >> 16) & 1)) & 0xFFFF0000
        parts.append(struct.unpack("<f", struct.pack("<I", u))[0])
        v -= parts[-1]
    return parts


ROOT_PARTS = bf16_parts(struct.unpack("<f", struct.pack("<f", ROOT))[0])


def gnn_kernel(nc, a_blocks, xt, wcat, consts, tri, out):
    with ExitStack() as ctx:
        def sb(name, shape, dt=F32):
            return ctx.enter_context(nc.sbuf_tensor(name, shape, dt))

        def sem(name):
            return ctx.enter_context(nc.semaphore(name))

        slots = sb("slots", [P, HB * SLOT])
        REGION = NB * D
        work = sb("work", [P, 5 * REGION])
        cst = sb("cst", [P, NCONST])
        tri_sb = sb("tri_sb", [P, 3, P], BF16)
        stats = sb("stats", [P, NB, 6])
        small = sb("small", [P, 8, NB])
        cols = sb("cols", [P, 12])
        neg_rs = sb("neg_rs", [P, NB])
        flag_i = sb("flag_i", [1, 1], I32)
        banks = ctx.enter_context(nc.psum_tensor("banks", [P, 8, 512], F32))
        hbias = cols[:, 9:10]

        def const(name, rows=P):
            a, b = COLS[name]
            return cst[0:rows, a:b]

        ident = const("ident")

        a_slot = slots[:, :].rearrange("p (s j i) -> p s j i", s=HB, j=NB)
        a_flat = slots[:, :].rearrange("p (s w) -> p s w", s=HB)
        xt_sb = slots[0:D + 1, (HB - 1) * SLOT:HB * SLOT]

        def words(a, n):
            return work[:, a:a + n]

        def region(n):
            return words((n + 1) * REGION, REGION)

        def halves(n):
            return region(n).rearrange("p (h w) -> p h w", h=2)

        def rows(n, h, s0, cnt):
            return halves(n)[:, h, s0 * D:(s0 + cnt) * D]

        def blocks(n):
            return region(n).rearrange("p (b c) -> p b c", c=D)

        doubled = words(0, REGION).rearrange("p (j c) -> p j c", c=D)
        wcat_sb = work[0:D + 1, 0:4 * D]
        u_all = words(REGION, 4 * REGION).rearrange("p (u b c) -> p u b c", u=4, c=D)
        XW3, XW2, XW1, XW0 = 0, 1, 2, 3
        X1, X2 = 1, 3
        yt_w = [max(cnt for _, cnt in CHUNKS[n::2]) * P for n in range(2)]
        yt = [words(REGION, yt_w[0]), words(REGION + yt_w[0], yt_w[1])]
        rsp = words(REGION + sum(yt_w), RS_RING * P).rearrange("p (b i) -> p b i", i=P)
        zx = words(0, 512).rearrange("p (b c) -> p b c", c=P)
        zxt = words(512, 512)
        ht = words(1024, 512)
        SPL_W = 3 * D // 2
        seven, ten = CHUNKS[2][0], CHUNKS[3][0]
        spl_at = {0: 3 * REGION, HB: 2 * REGION - seven * SPL_W, HB + seven: 3 * REGION + HB * SPL_W, HB + ten: 0}
        assert REGION + sum(yt_w) + seven * SPL_W <= 2 * REGION and (HB + ten - seven) * SPL_W <= REGION

        assert sum(yt_w) + RS_RING * P <= REGION

        def split_of(j, cnt=1):
            first = max(b for b in spl_at if b <= j)
            return words(spl_at[first] + (j - first) * SPL_W, cnt * SPL_W).bitcast(BF16).rearrange("p (j c) -> p j c", c=3 * D)

        at = (HB - ten) * SPL_W
        ci_buf = [words(at + 256 * n, 256).bitcast(BF16) for n in range(RING)]
        ci_zero = words(at + 256 * RING, 256).bitcast(BF16)
        at += 256 * (RING + 1)
        wt = [words(at + 256 * n, 256).bitcast(BF16) for n in range(RING)]
        assert at + 256 * RING <= spl_at[HB]
        oh, ol = words(2 * REGION, 512), words(2 * REGION + 512, 512)
        nf = words(0, NB * (D + 1)).rearrange("p (b c) -> p b c", c=D + 1)
        at = NB * (D + 1)
        v3 = words(at, REGION).rearrange("p (b c) -> p b c", c=D)
        at += REGION
        ot = words(at, 512)
        agg = words(at + 512, 4 * D).rearrange("p (b c) -> p b c", c=D)
        agg_flat = words(at + 512, 4 * D)
        tmp6 = words(at + 768, 4 * D).rearrange("p (b c) -> p b c", c=D)
        aggt = words(at + 1024, 2 * P)
        parts = words(at + 1280, NB * 6).bitcast(BF16).rearrange("p (b c) -> p b c", c=12)
        ex = words(at + 1440, 512)
        assert 1280 + NB * 6 <= 1440 and at + 1952 <= (X2 + 1) * REGION
        x3 = blocks(X2)
        SQUARES_AT = at + 1952
        assert SQUARES_AT + EARLY * D <= (X2 + 1) * REGION
        t8 = SLOTS6 * SLOT
        ua, ub, va, vb = (slots[0:k, t8 + n * SLOT // 2:t8 + (n + 1) * SLOT // 2].bitcast(BF16)
                          for n, k in enumerate((KA, KB, KA, KB)))
        nat_w = NB * HALF_NAT
        natural_f = slots[:, t8 + 2 * SLOT:t8 + 2 * SLOT + nat_w].bitcast(BF16).rearrange("p (b u c) -> p b u c", u=2, c=HALF_NAT)
        nu, nv = natural_f[:, :, 0, :], natural_f[:, :, 1, :]
        tiles5 = ((va, nu, 0, KA, -2.0), (ua, nv, 0, KA, 1.0), (ub, nu, D, KB, 1.0), (vb, nv, D, KB, -2.0))
        turns5 = [[(b0, tile) for b0 in range(0, NB, 8) for tile in pair] for pair in (tiles5[:2], tiles5[2:])]
        assert nat_w <= 2 * SLOT
        st = [slots[:, t8 + 2 * SLOT + 512 * n:t8 + 2 * SLOT + 512 * (n + 1)] for n in range(S_RING)]
        sq = [slots[:, t8 + 4 * SLOT + 512 * n:t8 + 4 * SLOT + 512 * (n + 1)] for n in range(2)]
        assert 512 * S_RING <= 2 * SLOT
        gen = [slots[:, t8 + 512 * n:t8 + 512 * (n + 1)] for n in range(12)]
        gen_s = gen[11]
        ut, vt, vt2 = (slots[0:NF, t8 + (2 + n) * SLOT:t8 + (3 + n) * SLOT] for n in range(3))
        gu = words(NB * (D + 1), NB * NF).rearrange("p (b c) -> p b c", c=NF)

        ld = [sem(f"slot_loaded{s}") for s in range(HB)]
        c_ld = sem("constants_loaded")
        x_ld = sem("xt_loaded")
        ld6 = sem("pass5_loaded")
        arrived = sem("blocks_arrived")
        u_ps = sem("xw_in_psum")
        u_sb = sem("xw_in_sbuf")
        doubled_r = sem("first_operand_ready")
        x1_rdy = sem("x1_ready")
        nrm_r = sem("early_norm_ready")
        pl = sem("pool_chain")
        inv_r = sem("inverse_root_ready")
        prod = sem("chunk_product_done")
        y_rdy = sem("product_in_sbuf")
        bk = sem("product_turned_back")
        freed = sem("chunk_read")
        rs_sum = sem("partial_row_sums")
        rs_ps = sem("row_sums_in_psum")
        link = sem("vector_chain")
        ln_c = sem("norm_chain")
        ve = sem("variance_ready")
        rt = sem("root_ready")
        zx_r, t4, c4, h4, a4, y4 = (sem(f"comm_{n}") for n in ("features", "turned", "turned_in_sbuf", "hidden", "tanh", "read"))
        spl_rdy = sem("split_ready")
        ci = sem("suffix_masks_built")
        c_done = sem("counts_done")
        w_rdy = sem("weights_ready")
        w_used = sem("weights_used")
        c5, o5, y5 = (sem(f"decay_{n}") for n in ("sum_in_sbuf", "out", "out_read"))
        pm_t = sem("deviation_ready")
        pm_r = sem("deviation_turned")
        fl_i = sem("flag_ready")
        nat = sem("features_ready")
        ft_t = sem("features_turned")
        ft_c = sem("features_copied")
        ft_v = sem("features_copied_vector")
        g_done = sem("forms_done")
        q_done = sem("squares_done")
        t_rdy = sem("weights_before_a")
        sd_rdy = sem("s_ready_vector")
        sp_rdy = sem("s_ready_pool")
        s_used = sem("s_used")
        gl = sem("gather_chain")
        gc = sem("general_chain")
        ga = sem("general_act_done")
        gv = sem("general_act_input")
        e6, b6, z6, t6, c6, o6, y6 = (sem(f"ball_{n}") for n in (
            "sum_in_sbuf", "sum_turned", "agg_ready", "agg_turned", "turned_in_sbuf", "out", "out_read"))
        a_used = sem("pass5_chunk_used")
        th = sem("act_result_ready")
        vr = sem("act_input_ready")
        fin = sem("final_chain")
        stored = sem("stored")

        block = ctx.enter_context(nc.Block())

        @block.sync
        def _(sp):
            sp.dma_start(xt_sb, xt).then_inc(x_ld, 16)
            sp.dma_start(wcat_sb, wcat).then_inc(x_ld, 16)
            sp.dma_start(cst[:, :], consts).then_inc(c_ld, 16)
            sp.dma_start(tri_sb[:, :, :], tri).then_inc(c_ld, 16)
            for s in range(HB):
                if s == HB - 1:
                    sp.wait_ge(u_ps, NB)
                sp.dma_start(a_flat[:, s], a_blocks[HB + s]).then_inc(ld[s], 16)
            for c, (s0, cnt) in enumerate(CHUNKS):
                for s in range(s0, s0 + cnt):
                    sp.wait_ge(prod, c + 1)
                    sp.wait_ge(rs_sum, s + 1)
                    sp.dma_start(a_flat[:, s], a_blocks[s]).then_inc(ld[s], 16)
            with sp.Fori(2, 5) as g:
                for c, (s0, cnt) in enumerate(CHUNKS):
                    for s in range(s0, s0 + cnt):
                        sp.wait_ge(prod, g * (2 * NC) + (c + 1 - 2 * NC))
                        sp.wait_ge(rs_sum, HB + s + 1)
                        sp.dma_start(a_flat[:, s], a_blocks[((g + 1) % 2) * HB + s]).then_inc(ld[s], 16)
            for c, (s0, cnt) in enumerate(CHUNKS):
                for s in range(s0, s0 + cnt):
                    sp.wait_ge(ci, 2 * NB * (c + 1))
                    sp.dma_start(a_flat[:, s], a_blocks[s]).then_inc(ld[s], 16)
            wide = slots[:, 0:SLOTS6 * SLOT].rearrange("p (t w) -> p t w", t=2)
            with sp.Fori(2, FULL6) as t:
                sp.wait_ge(a_used, t - 1)
                src = a_blocks[0:FULL6 * STEP6].rearrange("(t b) p w -> t p b w", b=STEP6)
                sp.dma_start(wide[:, t % 2].rearrange("p (b w) -> p b w", b=STEP6), src[t]).then_inc(ld6, 16)
                sp.wait_ge(ld6, 16 * t - 16)
                sp.sem_inc(arrived, 1)
            sp.wait_ge(a_used, FULL6 - 1)
            sp.dma_start(a_flat[:, 0:REST6, :] if FULL6 % 2 == 0 else a_flat[:, STEP6:STEP6 + REST6, :],
                         a_blocks[FULL6 * STEP6:NB].rearrange("b p w -> p b w")).then_inc(ld6, 16)
            sp.wait_ge(ld6, 16 * (FULL6 - 1))
            sp.sem_inc(arrived, 1)
            by_rows = out[0:(NB - 1) * P].rearrange("(b p) c -> p b c", p=P)
            sp.wait_ge(fin, FIN_STEPS)
            sp.dma_start(by_rows[:, 0:EARLY, :], v3[:, 0:EARLY, :]).then_inc(stored, 16)
            sp.wait_ge(fin, 2 * FIN_STEPS)
            sp.dma_start(by_rows[:, EARLY:, :], v3[:, EARLY:NB - 1, :]).then_inc(stored, 16)
            sp.dma_start(out[(NB - 1) * P:N], v3[0:N - (NB - 1) * P, NB - 1, :]).then_inc(stored, 16)
            sp.wait_ge(stored, 48)

        def a6(par, jb, cnt):
            return a_slot[:, par * STEP6:par * STEP6 + cnt, jb, :]

        def split(ap, cnt):
            return ap[:, 0:cnt * P].rearrange("p (b i) -> p b i", i=P)

        def over_chunks(eng, body):
            body(0, 0, STEP6, True, STEP6)
            with eng.Fori(0, FULL6 // 2 - 1) as pair:
                body(pair * 2 + 1, 1, STEP6, False, STEP6)
                body(pair * 2 + 2, 0, STEP6, False, STEP6)
            body(FULL6 - 1, 1, STEP6, False, REST6)
            body(FULL6, 0, REST6, False, 0)

        def turned5(stage, n, rows):
            return banks[0:rows, 2 * stage + n % 2, :].bitcast(BF16)

        def is_early(t):
            return isinstance(t, int) and t == EARLY_CHUNK

        def form_bank(par, jb):
            return 4 + (par * NB + jb) % RING

        @block.gpsimd
        def _(pool):
            with pool.Fori(0, 6) as g:
                for s in range(HB):
                    pool.wait_ge(ld[s], 16 * g + 16)
                    pool.sem_inc(arrived, 1)
            n = [0]

            def step(ins):
                n[0] += 1
                ins.then_inc(pl, 1)
                pool.wait_ge(pl, n[0])

            def add_up(dst, wide, a):
                w = D // 2
                step(pool.tensor_tensor(wide[:, :, 0:w], a[:, :, 0:w], a[:, :, w:2 * w], ALU.add))
                while w > 2:
                    w //= 2
                    step(pool.tensor_tensor(wide[:, :, 0:w], wide[:, :, 0:w], wide[:, :, w:2 * w], ALU.add))
                step(pool.tensor_tensor(dst, wide[:, :, 0], wide[:, :, 1], ALU.add))

            def temporary(m, w):
                return words(2 * REGION + 1024, m * w).rearrange("p (b c) -> p b c", c=w)

            def squares_of(dst, x):
                blocks_ = x.shape[1]
                for first in range(0, blocks_, 10):
                    m = min(10, blocks_ - first)
                    sq = temporary(m, D)
                    step(pool.tensor_tensor(sq, x[:, first:first + m, :], x[:, first:first + m, :], ALU.mult))
                    add_up(dst[:, first:first + m], sq, sq)

            for nth, (b0, b1, _, _) in enumerate(EARLY_NORMS):
                x = x3[:, b0:b1, :]
                nrm, sums, var, mean, rec = (small[:, i, b0:b1] for i in (0, 1, 2, 3, 4))
                pool.wait_ge(y5, 2 + NC + 2 * nth)
                add_up(sums, temporary(b1 - b0, D // 2), x)
                step(pool.tensor_scalar(mean, sums, 1.0 / D, None, ALU.mult))
                step(pool.tensor_tensor(x, x, mean.unsqueeze(2).to_broadcast([P, b1 - b0, D]), ALU.subtract))
                squares_of(var, x)
                step(pool.tensor_scalar(var, var, 0.25 / D, EPS / 4, ALU.mult, ALU.add))
                pool.sem_inc(ve, 1)
                pool.wait_ge(inv_r, nth + 1)
                step(pool.tensor_tensor(x, x, rec.unsqueeze(2).to_broadcast([P, b1 - b0, D]), ALU.mult))
                squares_of(nrm, x)
                pool.sem_inc(nrm_r, 1)

            pool.wait_ge(fl_i, 1)
            fast = pool.value_load(flag_i[0:1, 0:1], min_val=0, max_val=1)

            def weighted(t, par, cnt, first, nxt):
                for jb in range(NB):
                    if not ON_POOL[jb]:
                        continue
                    pool.wait_ge(arrived, t + (6 * HB - 1))
                    pool.wait_ge(t_rdy, t * NB + (RING + jb + 1))
                    s = split(st[jb % S_RING], cnt)
                    nc.gpsimd.tensor_tensor(s, s, a6(par, jb, cnt), ALU.mult).then_inc(sp_rdy, 1)

            with pool.If(fast != 0):
                over_chunks(pool, weighted)
            with pool.Else():
                pool.wait_ge(fl_i, 1)

        @block.tensor
        def _(pe):
            pe.wait_ge(x_ld, 32)
            pe.wait_ge(c_ld, 32)
            for b in range(NB):
                if b >= RING:
                    pe.wait_ge(u_sb, b - RING + 2)
                o = banks[:, b % RING, 0:4 * D]
                pe.matmul(o, xt_sb[:, b * P:(b + 1) * P], wcat_sb, start=True, stop=False)
                pe.matmul(o[:, 3 * D:4 * D], xt_sb[:, b * P:(b + 1) * P], const("ident", D + 1)[:, 0:D],
                          start=False, stop=True).then_inc(u_ps, 1)

            def product(n, c, k_arrived, operand, order, ready, between):
                s0, cnt = CHUNKS[c]
                pe.wait_ge(arrived, k_arrived + (s0 + cnt))
                pe.wait_ge(y_rdy, n + 1)
                for h in range(PAIRS):
                    if h in between:
                        between[h]()
                    for side in range(2):
                        at = 2 * h + side
                        if at in ready:
                            pe.wait_ge(*ready[at])
                        last = pe.matmul(banks[side * D:(side + 1) * D, c % 2, 0:cnt * P], operand[:, order[at], :],
                                         a_slot[:, s0:s0 + cnt, order[at], :], start=(h == 0), stop=(h == PAIRS - 1))
                last.then_inc(prod, 1)

            def back(n, c):
                pe.wait_ge(y_rdy, n + 3)
                pe.wait_ge(freed, n + 1)
                for i in range(CHUNKS[c][1]):
                    last = pe.matmul(banks[:, 2 + c % 2, i * D:(i + 1) * D], yt[c % 2][:, i * P:(i + 1) * P],
                                     const("fold"), start=True, stop=True)
                last.then_inc(bk, 1)

            def row_sums(k, c):
                first = (1 - k) * HB
                for s in range(CHUNKS[c][0], CHUNKS[c][0] + CHUNKS[c][1]):
                    pe.wait_ge(rs_sum, k * HB + (s + 1))
                    pe.matmul(banks[:, 4, first + s:first + s + 1], rsp[:, rs_buf(s), :], const("one"), start=True, stop=True)\
                        .then_inc(rs_ps, 1)

            first_half, second_half = list(range(HB)), list(range(HB, NB))

            def chunks_ready(signal, base):
                return {0: (signal, base + NC)} | {HB + s0: (signal, base + (NC + 1 + c)) for c, (s0, _) in enumerate(CHUNKS)}

            def last_chunk(c):
                return (c - 1) % NC

            pe.wait_ge(doubled_r, 1)
            for k in range(2):
                for c in range(NC):
                    n = k * NC + c
                    between = {}
                    if n:
                        between[4] = lambda n=n, c=c: back(n - 1, last_chunk(c))
                        between[9] = lambda n=n: row_sums(*divmod(n - 1, NC))
                    product(n, c, k * HB, doubled, first_half + second_half, {}, between)
            for p, src, order in ((1, XW2, second_half + first_half), (2, XW1, first_half + second_half)):
                with pe.Fori(0, 2) as k:
                    for c in range(NC):
                        n = k * NC + (p * 2 * NC + c)
                        product(n, c, k * HB + p * HB, blocks(src), order,
                                chunks_ready(freed, 2 + 2 * NC * (p - 1)) if c == 0 else {},
                                {4: lambda n=n, c=c: back(n - 1, last_chunk(c))})
                if p == 1:
                    row_sums(1, NC - 1)

            def turn4(m, c):
                pe.wait_ge(zx_r, m + 1)
                pe.wait_ge(c4, m + 1)
                for i in range(CHUNKS[c][1]):
                    last = pe.transpose(banks[:, 4, i * P:(i + 1) * P], zx[:, i, :], ident)
                last.then_inc(t4, 1)

            def hidden4(m, c):
                w = CHUNKS[c][1] * P
                pe.wait_ge(c4, m + 2)
                pe.wait_ge(a4, m + 1)
                pe.matmul(banks[:, 5, 0:w], const("w1")[D:2 * D, :], zxt[D:2 * D, 0:w], start=True, stop=True)\
                    .then_inc(h4, 1)

            def sum4(m, c):
                pe.wait_ge(y_rdy, m + (6 * NC + 3))
                pe.wait_ge(a4, m + 2)
                pe.wait_ge(y4, m + 1)
                for i in range(CHUNKS[c][1]):
                    o = banks[:, 6 + c % 2, i * D:(i + 1) * D]
                    pe.matmul(o, yt[c % 2][:, i * P:(i + 1) * P], const("bt"), start=True, stop=False)
                    pe.matmul(o, zxt[:, i * P:(i + 1) * P], const("qb"), start=False, stop=False)
                    last = pe.matmul(o, ht[:, i * P:(i + 1) * P], const("w2"), start=False, stop=True)
                last.then_inc(bk, 1)

            for m in range(2 * NC):
                k, c = divmod(m, NC)
                between = {9: lambda m=m, c=c: turn4(m, c), 11: lambda m=m, c=c: hidden4(m, c)}
                if m:
                    between[2] = lambda m=m, c=c: sum4(m - 1, last_chunk(c))
                else:
                    between[4] = lambda: back(6 * NC - 1, NC - 1)
                product(m + 6 * NC, c, k * HB + 3 * HB, blocks(X1), second_half + first_half,
                        chunks_ready(x1_rdy, 0) if m == 0 else {}, between)
            sum4(2 * NC - 1, NC - 1)

            def counts(n, c, i):
                k4 = n * NB + i
                g = c * NB + i
                w = CHUNKS[c][1] * P
                pe.wait_ge(ci, 2 * k4 + 2)
                pe.wait_ge(w_rdy, k4 + 1)
                o = banks[:, 4 + g % RING, 0:w]
                pe.matmul(o, tri_sb[:, 0, :], ci_buf[g % RING][:, 0:w], start=True, stop=False)
                later = ci_buf[(g - 1) % RING] if i else ci_zero
                pe.matmul(o, tri_sb[:, 1, :], later[:, 0:w], start=False, stop=True).then_inc(c_done, 1)

            def neighbours(n, c, i):
                w = CHUNKS[c][1] * P
                k4 = n * NB + i
                pe.wait_ge(w_rdy, k4 + (RING + 2))
                if i == 0:
                    pe.wait_ge(c5, n + 1)
                    pe.wait_ge(y5, n + 1)
                b = 2 * (c % 2)
                for t in range(2):
                    j = NB - 1 - (i + t)
                    pe.matmul(banks[:, b, 0:w], split_of(j)[:, 0, 0:2 * D], wt[(c * NB + i + t) % RING][:, 0:w],
                              start=(i + t == 0), stop=(i + t == NB - 1))
                for t in range(2):
                    j = NB - 1 - (i + t)
                    pe.matmul(banks[t * D:(t + 1) * D, b + 1, 0:w], split_of(j)[:, 0, 2 * D:3 * D],
                              wt[(c * NB + i + t) % RING][:, 0:w], start=(i == 0), stop=(i == NB - 2)).then_inc(w_used, 1)

            def out5(n, c):
                pe.wait_ge(c5, n + 3)
                for i in range(CHUNKS[c][1]):
                    o = banks[:, 2 * (c % 2), i * D:(i + 1) * D]
                    pe.matmul(o, oh[:, i * P:(i + 1) * P], const("lw2"), start=True, stop=False)
                    last = pe.matmul(o, ol[:, i * P:(i + 1) * P], const("lw2"), start=False, stop=True)
                last.then_inc(o5, 1)

            with pe.Fori(0, 2) as k:
                steps = [(c, i) for c in range(NC) for i in range(NB)]
                for c, i in steps[:2]:
                    counts(k * NC + c, c, i)
                pe.wait_ge(spl_rdy, 2 * NC)
                for g in range(0, len(steps), 2):
                    for c, i in steps[g + 2:g + 4]:
                        counts(k * NC + c, c, i)
                    c, i = steps[g]
                    if i == 6:
                        if c:
                            out5(k * NC + (c - 1), c - 1)
                        else:
                            with pe.If(k != 0):
                                out5(k * NC - 1, NC - 1)
                    neighbours(k * NC + c, c, i)
            out5(2 * NC - 1, NC - 1)

            pe.wait_ge(pm_t, 1)
            pe.transpose(banks[0:1, 2, 0:P], cols[:, 0:1], ident).then_inc(pm_r, 1)
            pe.wait_ge(fl_i, 1)
            fast = pe.value_load(flag_i[0:1, 0:1], min_val=0, max_val=1)

            def aggregate(par, cnt, jb, s):
                side = jb % 2
                pe.matmul(banks[side * D:(side + 1) * D, par, 0:cnt * P], nf[:, jb, 0:D], s[:, 0:cnt * P],
                          start=(jb < 2), stop=(jb >= NB - 2))

            def last_column(cnt, jb, s):
                q = jb % 4
                pe.matmul(banks[q * QUARTER:(q + 1) * QUARTER, 3, 0:cnt * P], nf[:, jb, D + 1 - QUARTER:D + 1],
                          s[:, 0:cnt * P], start=(jb < 4), stop=(jb >= NB - 4)).then_inc(s_used, 1)

            def back6(t, cnt):
                pe.wait_ge(e6, t + 3)
                for i in range(cnt):
                    at = i * (D + 1)
                    pe.matmul(banks[:, 2, at:at + D], ot[:, i * P:(i + 1) * P], const("fold"), start=True, stop=True)
                    last = pe.matmul(banks[:, 2, at + D:at + D + 1], ex[:, i * P:(i + 1) * P], const("sel"),
                                     start=True, stop=True)
                last.then_inc(b6, 1)

            def turn6(t, cnt):
                pe.wait_ge(z6, t + 1)
                for i in range(cnt // 2):
                    last = pe.transpose(banks[:, 2, i * P:(i + 1) * P], agg_flat[:, i * P:(i + 1) * P], ident)
                last.then_inc(t6, 1)

            def out6(t, cnt):
                pe.wait_ge(c6, t + 1)
                for i in range(cnt // 2):
                    last = pe.matmul(banks[:, 2, i * P:(i + 1) * P], aggt[:, i * P:(i + 1) * P], const("lw3"),
                                     start=True, stop=True)
                last.then_inc(o6, 1)

            def chunk_of(v, t, w):
                if isinstance(t, int):
                    return v[:, t * STEP6 * P:t * STEP6 * P + w]
                return v[:, 0:FULL6 * STEP6 * P].rearrange("p (t w) -> p t w", t=FULL6)[:, t, :]

            def forms(t, par, cnt, jb):
                pe.wait_ge(t_rdy, t * NB + (jb + 1))
                o = banks[:, form_bank(par, jb), 0:cnt * P]
                pe.matmul(o, ua[:, jb * P:(jb + 1) * P], chunk_of(va, t, cnt * P), start=True, stop=False)
                pe.matmul(o, ub[:, jb * P:(jb + 1) * P], chunk_of(vb, t, cnt * P), start=False, stop=True)\
                    .then_inc(g_done, 1)

            def near(t, par, cnt, first, nxt):
                for jb in range(NB):
                    if jb + AHEAD6 < NB:
                        forms(t, par, cnt, jb + AHEAD6)
                    elif nxt:
                        forms(t + 1, 1 - par, nxt, jb + AHEAD6 - NB)
                    if not first:
                        if jb == 5:
                            back6(t - 1, STEP6)
                        if jb == 12:
                            turn6(t - 1, STEP6)
                        if jb == 16:
                            out6(t - 1, STEP6)
                    if jb == 0:
                        pe.wait_ge(e6, t + 1)
                    done = sum(ON_POOL[:jb + 1])
                    if ON_POOL[jb]:
                        pe.wait_ge(sp_rdy, t * sum(ON_POOL) + done)
                    else:
                        pe.wait_ge(sd_rdy, t * (NB - sum(ON_POOL)) + (jb + 1 - done))
                    aggregate(par, cnt, jb, st[jb % S_RING])
                    if jb % 4 == 3 or jb == NB - 1:
                        if jb == 3:
                            pe.wait_ge(e6, t + 2)
                        for b in range(jb // 4 * 4, jb + 1):
                            last_column(cnt, b, st[b % S_RING])

            with pe.If(fast != 0):
                for stage, copied in enumerate((ft_c, ft_v)):
                    pe.wait_ge(nat, stage + 1)
                    for n, (b0, (_, src, off, k, _)) in enumerate(turns5[stage]):
                        pe.wait_ge(copied, n + RING - 1)
                        for b in range(b0, min(b0 + 8, NB)):
                            last = pe.transpose(turned5(stage, n, k)[:, (b - b0) * P:(b - b0 + 1) * P],
                                                src[:, b, off:off + k], tri_sb[:, 2, :])
                        last.then_inc(ft_t, 1)
                pe.wait_ge(ft_c, RING + len(turns5[0]))
                pe.wait_ge(ft_v, RING + len(turns5[1]))
                for jb in range(AHEAD6):
                    forms(0, 0, STEP6, jb)
                over_chunks(pe, near)
            with pe.Else():
                turned = 0
                for rnd in range(3):
                    pe.wait_ge(nat, rnd + 1)
                    for b0 in range(0, NB, 4):
                        pe.wait_ge(ft_c, turned + 1)
                        for b in range(b0, min(b0 + 4, NB)):
                            last = pe.transpose(banks[0:NF, 4 + turned % RING, (b - b0) * P:(b - b0 + 1) * P],
                                                gu[:, b, :], ident)
                        last.then_inc(ft_t, 1)
                        turned += 1
                pe.wait_ge(ft_c, RING + turned)

                def general(t, par, cnt, first, nxt):
                    for jb in range(NB):
                        pe.wait_ge(t_rdy, t * NB + (jb + RING))
                        for b, v in ((4, vt), (5, vt2)):
                            ins = pe.matmul(banks[:, b, 0:cnt * P], ut[:, jb * P:(jb + 1) * P], chunk_of(v, t, cnt * P),
                                            start=True, stop=True)
                        ins.then_inc(g_done, 1)
                        if not first:
                            if jb == 5:
                                back6(t - 1, STEP6)
                            if jb == 12:
                                turn6(t - 1, STEP6)
                            if jb == 16:
                                out6(t - 1, STEP6)
                        pe.wait_ge(t_rdy, t * NB + (jb + RING + 1))
                        if jb == 0:
                            pe.wait_ge(e6, t + 2)
                        aggregate(par, cnt, jb, gen_s)
                        last_column(cnt, jb, gen_s)

                over_chunks(pe, general)
            back6(FULL6, REST6)
            turn6(FULL6, REST6)
            out6(FULL6, REST6)

        @block.scalar
        def _(act):
            for b in range(0, NB, 2):
                act.wait_ge(u_ps, b + 1)
                act.wait_ge(u_sb, b + 1)
                act.copy(u_all[:, :, b, :], banks[:, b % RING, 0:4 * D].rearrange("p (u c) -> p u c", u=4)).then_inc(u_sb, 1)

            def to_sbuf(n, c):
                w = CHUNKS[c][1] * P
                act.wait_ge(prod, n + 1)
                act.wait_ge(bk, n + 1)
                act.copy(yt[c % 2][:, 0:w], banks[:, c % 2, 0:w]).then_inc(y_rdy, 1)

            def root(nb, b0=0):
                act.activation(small[:, 3, b0:b0 + nb], small[:, 2, b0:b0 + nb], ACT.Sqrt).then_inc(rt, 1)

            act.wait_ge(doubled_r, 1)
            with act.Fori(0, 4) as half:
                for c in range(NC):
                    to_sbuf(half * NC + c, c)
            with act.Fori(0, 2) as k:
                for c in range(NC):
                    to_sbuf(k * NC + (4 * NC + c), c)
                    act.wait_ge(ve, k * NC + (c + 1))
                    root(CHUNKS[c][1])

            def turned4(m, c):
                w = CHUNKS[c][1] * P
                act.wait_ge(t4, m + 1)
                act.wait_ge(bk, m + (6 * NC + 2))
                act.copy(zxt[:, 0:w], banks[:, 4, 0:w]).then_inc(c4, 1)

            def tanh4(m, c):
                w = CHUNKS[c][1] * P
                act.wait_ge(h4, m + 1)
                act.activation(ht[:, 0:w], banks[:, 5, 0:w], ACT.Tanh, bias=hbias).then_inc(a4, 1)

            with act.Fori(0, 2) as k:
                for c in range(NC):
                    turned4(k * NC + c, c)
                    tanh4(k * NC + c, c)
                    to_sbuf(k * NC + (6 * NC + c), c)
                    act.wait_ge(ve, k * NC + (2 * NC + c + 1))
                    root(CHUNKS[c][1])

            def weights(n, c, i):
                k4 = n * NB + i
                g = c * NB + i
                w = CHUNKS[c][1] * P
                act.wait_ge(c_done, k4 + 4)
                act.wait_ge(w_used, k4 + 1)
                act.activation(wt[g % RING].bitcast(U16)[:, 0:w], banks[:, 4 + g % RING, 0:w], ACT.Relu,
                               bias=cols[:, 11:12]).then_inc(w_rdy, 1)

            def sums5(n, c):
                w = CHUNKS[c][1] * P
                act.wait_ge(w_used, n * NB + (RING + NB))
                act.wait_ge(o5, n + 1)
                act.mul(oh[:, 0:w], banks[:, 2 * (c % 2), 0:w], UNSCALE)
                act.mul(ol[:, 0:w], banks[:, 2 * (c % 2) + 1, 0:w], UNSCALE).then_inc(c5, 1)

            with act.Fori(0, 2) as k:
                for c in range(NC):
                    for i in range(NB):
                        weights(k * NC + c, c, i)
                        if i == 3:
                            if c:
                                sums5(k * NC + (c - 1), c - 1)
                            else:
                                with act.If(k != 0):
                                    sums5(k * NC - 1, NC - 1)
                        for nth, (b0, b1, at, _) in enumerate(EARLY_NORMS):
                            if (c, i) == at:
                                with act.If(k != 0):
                                    act.wait_ge(ve, 4 * NC + 1 + nth)
                                    root(b1 - b0, b0)
            sums5(2 * NC - 1, NC - 1)
            act.wait_ge(ve, 4 * NC + 3)
            root(HB - LATE0, LATE0)

            act.wait_ge(fl_i, 1)
            fast = act.value_load(flag_i[0:1, 0:1], min_val=0, max_val=1)

            def sums6(t, par, cnt):
                act.wait_ge(s_used, t * NB + (S_RING + NB))
                act.wait_ge(b6, t + 1)
                act.copy(ot[:, 0:cnt * P], banks[:, par, 0:cnt * P])
                act.copy(ex[:, 0:cnt * P], banks[:, 3, 0:cnt * P]).then_inc(e6, 1)

            def turned6(t, cnt):
                act.wait_ge(t6, t + 1)
                act.copy(aggt[:, 0:cnt // 2 * P], banks[:, 2, 0:cnt // 2 * P]).then_inc(c6, 1)

            def final_acts(nth, nb):
                act.wait_ge(vr, 2 * nth + 1)
                act.activation(small[:, 1, 0:nb], small[:, 0, 0:nb], ACT.Sqrt).then_inc(th, 1)
                yield
                act.wait_ge(vr, 2 * nth + 2)
                act.activation(small[:, 5, 0:nb], small[:, 4, 0:nb], ACT.Tanh).then_inc(th, 1)
                yield
                act.wait_ge(ve, 4 * NC + (4 + nth))
                root(nb)

            def squares(t, par, cnt, first, nxt):
                early = final_acts(0, EARLY)
                for jb in range(NB):
                    w = cnt * P
                    act.wait_ge(g_done, t * NB + (jb + 1))
                    act.wait_ge(t_rdy, t * NB + (jb + RING - 1))
                    act.activation(sq[jb % 2][:, 0:w], banks[:, form_bank(par, jb), 0:w], ACT.Square,
                                   bias=cols[:, 10:11]).then_inc(q_done, 1)
                    if not first and jb == AHEAD6:
                        sums6(t - 1, 1 - par, STEP6)
                    if not first and jb == 19:
                        turned6(t - 1, STEP6)
                    if is_early(t) and jb in (7, 9, 20):
                        next(early, None)

            with act.If(fast != 0):
                for n, (b0, (dst, _, _, k, factor)) in enumerate(turns5[0]):
                    w = min(8, NB - b0) * P
                    act.wait_ge(ft_t, n + 1)
                    act.mul(dst[:, b0 * P:b0 * P + w], turned5(0, n, k)[:, 0:w], factor).then_inc(ft_c, 1)
                over_chunks(act, squares)
            with act.Else():
                turned = 0
                for dst in (ut, vt, vt2):
                    for b0 in range(0, NB, 4):
                        w = min(4, NB - b0) * P
                        act.wait_ge(ft_t, turned + 1)
                        act.copy(dst[:, b0 * P:b0 * P + w], banks[0:NF, 4 + turned % RING, 0:w]).then_inc(ft_c, 1)
                        turned += 1

                def general(t, par, cnt, first, nxt):
                    with act.Fori(0, NB) as jb:
                        w = cnt * P
                        it = t * NB + jb
                        act.wait_ge(gv, 2 * it + 1)
                        act.activation(gen[3][:, 0:w], gen[2][:, 0:w], ACT.Sqrt).then_inc(ga, 1)
                        act.wait_ge(gv, 2 * it + 2)
                        act.activation(gen[5][:, 0:w], gen[4][:, 0:w], ACT.Ln, bias=1.0, scale=1.0)
                        act.activation(gen[6][:, 0:w], gen[4][:, 0:w], ACT.Ln, bias=1.0, scale=-1.0).then_inc(ga, 1)
                        if not first:
                            with act.If(jb == 0):
                                sums6(t - 1, 1 - par, STEP6)
                            with act.Else():
                                act.wait_ge(fl_i, 1)
                            with act.If(jb == 13):
                                turned6(t - 1, STEP6)
                            with act.Else():
                                act.wait_ge(fl_i, 1)

                over_chunks(act, general)
                for _ in final_acts(0, EARLY):
                    pass
            sums6(FULL6, FULL6 % 2, REST6)
            turned6(FULL6, REST6)
            for _ in final_acts(1, NB - EARLY):
                pass

        @block.vector
        def _(dve):
            linked = [0]

            def chain(ins):
                linked[0] += 1
                ins.then_inc(link, 1)
                dve.wait_ge(link, linked[0])

            for s, n in ((u_sb, 1), (y_rdy, 2), (bk, 2), (freed, 2), (c4, 1), (a4, 1), (y4, 2), (c_done, 3), (w_rdy, RING),
                         (w_used, RING), (c5, 2), (o5, 1), (y5, 2), (ft_c, RING), (ft_v, RING), (t_rdy, RING), (s_used, S_RING),
                         (e6, 2), (b6, 1), (rs_ps, RS_RING)):
                dve.sem_inc(s, n)
            chain(dve.memset(cols[:, 11:12], MASK_BIAS))
            chain(dve.memset(cols[:, 10:11], ROOT - MID))
            dve.wait_ge(c_ld, 32)
            chain(dve.tensor_scalar(hbias, const("w1t"), const("tcol"), const("b1"), ALU.mult, ALU.add))
            for b in range(1, NB, 2):
                dve.wait_ge(u_ps, b + 1)
                dve.wait_ge(u_sb, b + 1)
                dve.tensor_copy(u_all[:, :, b, :], banks[:, b % RING, 0:4 * D].rearrange("p (u c) -> p u c", u=4)).then_inc(u_sb, 1)
            dve.wait_ge(u_sb, NB + 1)
            dve.tensor_tensor(region(XW1), region(XW1), region(XW3), ALU.subtract)
            dve.tensor_scalar(words(0, REGION), region(XW3), 2.0, None, ALU.mult).then_inc(doubled_r, 1)
            chain(dve.tensor_scalar(region(XW2), region(XW2), 2.0, None, ALU.mult))
            dve.wait_ge(doubled_r, 1)

            def natural(c):
                return banks[:, 2 + c % 2, 0:CHUNKS[c][1] * D]

            def pass0(n, k, c):
                dve.wait_ge(bk, n + 3)
                o = rows(XW2, (k + 1) % 2, *CHUNKS[c])
                dve.scalar_tensor_tensor(o, natural(c), 2.0, o, ALU.mult, ALU.add).then_inc(freed, 1)

            with dve.Fori(0, 2) as k:
                for c, (s0, cnt) in enumerate(CHUNKS):
                    for s in range(s0, s0 + cnt):
                        dve.wait_ge(arrived, k * HB + (s + 1))
                        dve.wait_ge(rs_ps, k * HB + (s + 1 + (RS_RING - rs_gap(s))))
                        dve.tensor_reduce(rsp[:, rs_buf(s), :], a_slot[:, s, :, :].rearrange("p j i -> p i j"), AX_X, ALU.add)\
                            .then_inc(rs_sum, 1)
                    if c:
                        pass0(k * NC + (c - 1), k, c - 1)
                pass0(k * NC + (NC - 1), k, NC - 1)
            dve.wait_ge(freed, 2 + 2 * NC)
            chain(dve.scalar_tensor_tensor(region(XW0), region(XW2), -0.5, region(XW0), ALU.mult, ALU.add))

            with dve.Fori(0, 2) as k:
                for c in range(NC):
                    dve.wait_ge(bk, k * NC + (2 * NC + c + 3))
                    o = rows(XW1, k, *CHUNKS[c])
                    dve.tensor_tensor(o, natural(c), o, ALU.add).then_inc(freed, 1)
            dve.wait_ge(rs_ps, NB + RS_RING)
            chain(dve.tensor_scalar(neg_rs[:, :], banks[:, 4, 0:NB], -1.0, None, ALU.mult))

            def inverse_root(b0, b1, step):
                var, std, rec = (small[:, i, b0:b1] for i in (2, 3, 4))
                step(dve.reciprocal(rec, std))
                step(dve.tensor_tensor(rec, rec, var, ALU.mult))
                step(dve.tensor_tensor(std, std, rec, ALU.add))
                step(dve.reciprocal(rec, std))

            def norm(*args):
                for _ in norm_parts(*args):
                    pass

            def norm_parts(y, x, base, nb, roots, b0=0):
                n = [0]

                def step(ins):
                    n[0] += 1
                    ins.then_inc(ln_c, 1)
                    dve.wait_ge(ln_c, base + n[0])

                def col(i):
                    return stats[:, 0:nb, i]

                mean, dif, var, rec = (small[:, i, b0:b0 + nb] for i in (0, 1, 2, 4))
                dve.tensor_tensor(mean, col(1), col(4), ALU.add)
                dve.tensor_tensor(dif, col(1), col(4), ALU.subtract)
                step(dve.tensor_tensor(var, col(2), col(5), ALU.add))
                step(dve.tensor_scalar(mean, mean, 0.5, None, ALU.mult))
                step(dve.tensor_tensor(dif, dif, dif, ALU.mult))
                step(dve.scalar_tensor_tensor(var, dif, D / 4.0, var, ALU.mult, ALU.add))
                step(dve.tensor_scalar(var, var, 0.25 / D, EPS / 4, ALU.mult, ALU.add))
                dve.sem_inc(ve, 1)
                yield
                step(dve.tensor_tensor(x, y, mean.unsqueeze(2).to_broadcast([P, nb, D]), ALU.subtract))
                yield
                dve.wait_ge(rt, roots + 1)
                inverse_root(b0, b0 + nb, step)
                yield
                step(dve.tensor_tensor(x, x, rec.unsqueeze(2).to_broadcast([P, nb, D]), ALU.mult))
                assert n[0] == LN_STEPS

            def stats_of(ap, s0, cnt):
                for s in range(s0, s0 + cnt):
                    last = dve.bn_stats(stats[:, s, :], ap[:, (s - s0) * D:(s - s0 + 1) * D])
                return last

            def by_block(ap):
                return ap.rearrange("p (s c) -> p s c", c=D)

            with dve.Fori(0, 2) as k:
                h = (k + 1) % 2
                for c, (s0, cnt) in enumerate(CHUNKS):
                    dve.wait_ge(bk, k * NC + (4 * NC + c + 3))
                    y = rows(XW0, h, s0, cnt)
                    dve.tensor_tensor(y, natural(c), y, ALU.add).then_inc(freed, 1)
                    dve.wait_ge(freed, k * NC + (4 * NC + c + 3))
                    dve.tensor_copy(cols[:, 8:9], hbias)
                    stats_of(y, 0, cnt).then_inc(link, 1)
                    dve.wait_ge(link, k * NC + (linked[0] + c + 1))
                    norm(by_block(y), by_block(rows(X1, h, s0, cnt)), k * (NC * LN_STEPS) + c * LN_STEPS, cnt, k * NC + c)
                    dve.sem_inc(x1_rdy, 1)
            linked[0] += 2 * NC

            def features4(m):
                k, c = divmod(m, NC)
                s0, cnt = CHUNKS[c]
                dve.wait_ge(c4, m + 1)
                x = by_block(rows(X1, k, s0, cnt))
                rs = neg_rs[:, k * HB + s0:k * HB + s0 + cnt]
                dve.tensor_copy(zx[:, 0:cnt, D:2 * D], x)
                dve.tensor_tensor(zx[:, 0:cnt, 0:D], x, rs.unsqueeze(2).to_broadcast([P, cnt, D]), ALU.mult)\
                    .then_inc(zx_r, 1)

            features4(0)
            for m in range(2 * NC):
                k, c = divmod(m, NC)
                s0, cnt = CHUNKS[c]
                x2 = rows(X2, k, s0, cnt)
                dve.wait_ge(bk, m + (6 * NC + 3))
                dve.tensor_tensor(by_block(x2), by_block(banks[:, 6 + c % 2, 0:cnt * D]),
                                  const("b2").unsqueeze(1).to_broadcast([P, cnt, D]), ALU.add).then_inc(y4, 1)
                dve.wait_ge(y4, m + 3)
                chain(stats_of(x2, 0, cnt))
                norm(by_block(x2), by_block(x2), (2 * NC + m) * LN_STEPS, cnt, 2 * NC + m)
                if m + 1 < 2 * NC:
                    features4(m + 1)
                x2, parts4 = by_block(x2), split_of(k * HB + s0, cnt)
                chain(dve.tensor_copy(parts4[:, :, 0:D], x2))
                chain(dve.tensor_tensor(x2, x2, parts4[:, :, 0:D], ALU.subtract))
                chain(dve.tensor_copy(parts4[:, :, D:2 * D], x2))
                dve.tensor_tensor(parts4[:, :, 2 * D:3 * D], x2, parts4[:, :, D:2 * D], ALU.subtract).then_inc(spl_rdy, 1)
                dve.wait_ge(spl_rdy, m + 1)
                chain(dve.tensor_tensor(x2, x2, parts4[:, :, 0:D], ALU.add))
                chain(dve.tensor_tensor(x2, x2, const("lb2").unsqueeze(1).to_broadcast([P, cnt, D]), ALU.add))
            chain(dve.memset(ci_zero, 0.0))

            def masks(k, n, c, i):
                k4 = n * NB + i
                g = c * NB + i
                s0, cnt = CHUNKS[c]
                dve.wait_ge(c_done, k4 + 1)
                if i == 0:
                    dve.wait_ge(arrived, k * HB + (4 * HB + s0 + cnt))
                later = ci_buf[(g - 1) % RING] if i else ci_zero
                for part, (b, e) in enumerate(((0, 2), (2, cnt))):
                    if i:
                        dve.wait_ge(ci, 2 * k4 - 1 + part)
                    dve.scalar_tensor_tensor(split(ci_buf[g % RING], cnt)[:, b:e], a_slot[:, s0 + b:s0 + e, NB - 1 - i, :],
                                             0.0, split(later, cnt)[:, b:e], ALU.not_equal, ALU.add).then_inc(ci, 1)

            def read5(n, h, c):
                s0, cnt = CHUNKS[c]
                dve.wait_ge(o5, n + 2)
                o = rows(X2, h, s0, cnt)
                dve.tensor_tensor(o, banks[:, 2 * (c % 2), 0:cnt * D], o, ALU.add).then_inc(y5, 1)

            nrm = small[:, 0, :]

            with dve.Fori(0, 2) as k:
                for c in range(NC):
                    for i in range(NB):
                        masks(k, k * NC + c, c, i)
                        if i == 12:
                            if c:
                                read5(k * NC + (c - 1), (k + 1) % 2, c - 1)
                            else:
                                with dve.If(k != 0):
                                    read5(k * NC - 1, 1, NC - 1)
                        for nth, (b0, b1, _, at) in enumerate(EARLY_NORMS):
                            if (c, i) == at:
                                with dve.If(k != 0):
                                    dve.wait_ge(rt, 4 * NC + 1 + nth)
                                    inverse_root(b0, b1, chain)
                                    dve.sem_inc(inv_r, 1)
            read5(2 * NC - 1, 0, NC - 1)
            dve.wait_ge(y5, 2 + 2 * NC)
            late = HB - LATE0
            chain(stats_of(rows(X2, 0, LATE0, late), 0, late))
            dve.wait_ge(nrm_r, len(EARLY_NORMS))
            norm(x3[:, LATE0:HB, :], x3[:, LATE0:HB, :], 4 * NC * LN_STEPS, late, 4 * NC + 2, LATE0)
            squares = by_block(words(NB * (D + 1), late * D))
            chain(dve.tensor_tensor(squares, x3[:, LATE0:HB, :], x3[:, LATE0:HB, :], ALU.mult))
            chain(dve.tensor_reduce(nrm[:, LATE0:HB], squares, AX_X, ALU.add))

            nrm, bb, dev, mm, deg, beta, g1, bg1 = (small[:, i, :] for i in range(8))
            dve.tensor_scalar(bb, nrm, -1.0, 1.0, ALU.mult, ALU.add)
            chain(dve.tensor_scalar(dev, nrm, -float(D), None, ALU.add))
            chain(dve.scalar_tensor_tensor(dev, dev, -1.0, dev, ALU.mult, ALU.max))
            chain(dve.tensor_tensor(dev[:, NB - 1:NB], dev[:, NB - 1:NB], const("valid"), ALU.mult))
            dve.tensor_reduce(cols[:, 0:1], dev, AX_X, ALU.max).then_inc(pm_t, 1)
            dve.tensor_scalar(mm, bb, MIN_NORM, None, ALU.max)
            chain(dve.tensor_scalar(deg, neg_rs[:, :], -1.0, 1e-8, ALU.mult, ALU.max))
            dve.reciprocal(beta, bb)
            chain(dve.reciprocal(deg, deg))
            dve.wait_ge(pm_r, 1)
            chain(dve.tensor_reduce(cols[0:1, 1:2], banks[0:1, 2, 0:P], AX_X, ALU.max))
            chain(dve.tensor_scalar(cols[0:1, 2:3], cols[0:1, 1:2], NEAR, None, ALU.is_le))
            dve.tensor_copy(flag_i[:, :], cols[0:1, 2:3]).then_inc(fl_i, 1)
            dve.tensor_tensor(g1, mm, deg, ALU.mult)
            nb_ = dev
            dve.tensor_tensor(nf[:, :, 0:D], x3, beta.unsqueeze(2).to_broadcast([P, NB, D]), ALU.mult)
            chain(dve.tensor_tensor(nb_, nrm, beta, ALU.mult))
            chain(dve.tensor_tensor(nf[:, :, D], nb_, beta, ALU.add))
            dve.wait_ge(fl_i, 1)
            fast = dve.value_load(flag_i[0:1, 0:1], min_val=0, max_val=1)

            def some(t, cnt, ap, width):
                if isinstance(t, int):
                    return ap[:, t * STEP6 * width:(t * STEP6 + cnt) * width]
                return ap[:, 0:FULL6 * STEP6 * width].rearrange("p (t w) -> p t w", t=FULL6)[:, t, :]

            GATHER = 7

            def gather6(t, cnt):
                n = [0]

                def step(ins):
                    n[0] += 1
                    ins.then_inc(gl, 1)
                    dve.wait_ge(gl, t * GATHER + n[0])

                x = by_block(some(t, cnt, region(X2), D))
                o = banks[:, 2, 0:cnt * (D + 1)].rearrange("p (b c) -> p b c", c=D + 1)
                tmp, e = tmp6[:, 0:cnt, :], cols[:, 4:4 + cnt]
                dve.wait_ge(b6, t + 2)
                step(dve.tensor_tensor(tmp, o[:, :, 0:D], x, ALU.mult))
                step(dve.tensor_reduce(e, tmp, AX_X, ALU.add))
                step(dve.scalar_tensor_tensor(e, e, -2.0, o[:, :, D], ALU.mult, ALU.add))
                step(dve.tensor_tensor(e, e, some(t, cnt, g1, 1), ALU.mult))
                step(dve.tensor_tensor(tmp, x, e.unsqueeze(2).to_broadcast([P, cnt, D]), ALU.mult))
                step(dve.tensor_tensor(agg[:, 0:cnt, :], o[:, :, 0:D],
                                       some(t, cnt, bg1, 1).unsqueeze(2).to_broadcast([P, cnt, D]), ALU.mult))
                step(dve.tensor_tensor(agg[:, 0:cnt, :], agg[:, 0:cnt, :], tmp, ALU.subtract))
                dve.sem_inc(z6, 1)
                assert n[0] == GATHER

            def read6(t, cnt):
                dve.wait_ge(o6, t + 1)
                dve.tensor_tensor(by_block(some(t, cnt, words(NB * (D + 1), REGION), D)), by_block(banks[:, 2, 0:cnt * D]),
                                  const("lb3").unsqueeze(1).to_broadcast([P, cnt, D]), ALU.add).then_inc(y6, 1)

            def final_parts(b0, nb, nth, transformed):
                n = [nth * FIN_STEPS]

                def step(ins):
                    n[0] += 1
                    ins.then_inc(fin, 1)
                    dve.wait_ge(fin, n[0])

                ss, root, rec, vn, tanh = (small[:, i, 0:nb] for i in (0, 1, 2, 4, 5))
                v, x = v3[:, b0:b0 + nb, :], x3[:, b0:b0 + nb, :]
                v_flat = words(NB * (D + 1) + b0 * D, nb * D)
                dve.wait_ge(y6, transformed)
                sqo = by_block(words(SQUARES_AT, nb * D))
                step(dve.tensor_tensor(sqo, v, v, ALU.mult))
                yield
                step(dve.tensor_reduce(ss, sqo, AX_X, ALU.add))
                dve.sem_inc(vr, 1)
                yield
                dve.wait_ge(th, 2 * nth + 1)
                step(dve.tensor_scalar(root, root, MIN_NORM, None, ALU.max))
                step(dve.reciprocal(rec, root))
                step(dve.tensor_tensor(rec, rec, ss, ALU.mult))
                step(dve.tensor_tensor(vn, rec, root, ALU.add))
                step(dve.tensor_scalar(vn, vn, 0.5, MIN_NORM, ALU.mult, ALU.max))
                dve.sem_inc(vr, 1)
                yield
                step(dve.reciprocal(rec, vn))
                dve.wait_ge(th, 2 * nth + 2)
                step(dve.tensor_tensor(rec, rec, tanh, ALU.mult))
                step(dve.tensor_tensor(v, v, rec.unsqueeze(2).to_broadcast([P, nb, D]), ALU.mult))
                yield
                step(dve.tensor_tensor(v, v, x, ALU.add))
                yield
                step(stats_of(v_flat, 0, nb))
                yield
                yield from norm_parts(v, v, (4 * NC + 1 + nth) * LN_STEPS, nb, 4 * NC + 3 + nth)
                dve.sem_inc(fin, 1)
                assert n[0] + 1 == (nth + 1) * FIN_STEPS

            def near(t, par, cnt, first, nxt):
                early = final_parts(0, EARLY, 0, FULL6 - 2)

                def times_a(jb):
                    s = split(st[jb % S_RING], cnt)
                    dve.wait_ge(arrived, t + (6 * HB - 1))
                    dve.wait_ge(t_rdy, t * NB + (RING + jb + 1))
                    dve.tensor_tensor(s, s, a6(par, jb, cnt), ALU.mult).then_inc(sd_rdy, 1)

                for jb in range(NB):
                    w = cnt * P
                    dve.wait_ge(q_done, t * NB + (jb + 1))
                    dve.wait_ge(s_used, t * NB + (jb + 1))
                    dve.scalar_tensor_tensor(st[jb % S_RING][:, 0:w], sq[jb % 2][:, 0:w], FAR,
                                             banks[:, form_bank(par, jb), 0:w], ALU.add, ALU.mult).then_inc(t_rdy, 1)
                    if jb and not ON_POOL[jb - 1]:
                        times_a(jb - 1)
                    if jb == NB - 1 and not ON_POOL[jb]:
                        times_a(jb)
                    if not first:
                        if jb == 3:
                            dve.wait_ge(sd_rdy, t * (NB - sum(ON_POOL)))
                            dve.wait_ge(sp_rdy, t * sum(ON_POOL))
                            dve.sem_inc(a_used, 1)
                        if jb == 12:
                            gather6(t - 1, STEP6)
                        if jb == 23:
                            read6(t - 1, STEP6)
                    if is_early(t) and jb in (4, 6, 8, 10, 14, 16, 18, 20, 22, 24):
                        next(early, None)
                if is_early(t):
                    assert next(early, None) is None

            with dve.If(fast != 0):
                saved = linked[0]
                xb = nf[:, :, 0:D]
                chain(dve.tensor_copy(nu[:, :, 0:D], xb))
                dve.tensor_copy(nv[:, :, 0:D], nu[:, :, 0:D])
                dve.tensor_copy(nu[:, :, D:2 * D], nu[:, :, 0:D])
                dve.tensor_tensor(nv[:, :, D:2 * D], xb, nu[:, :, 0:D], ALU.subtract).then_inc(nat, 1)
                r = tmp6.rearrange("p b c -> p (b c)")[:, 0:NB]
                for at_, src in ((0, nb_), (3, beta)):
                    chain(dve.tensor_copy(parts[:, :, at_], src))
                    chain(dve.tensor_tensor(r, src, parts[:, :, at_], ALU.subtract))
                    chain(dve.tensor_copy(parts[:, :, at_ + 1], r))
                    chain(dve.tensor_tensor(parts[:, :, at_ + 2], r, parts[:, :, at_ + 1], ALU.subtract))
                dve.tensor_scalar(parts[:, :, 6:9], parts[:, :, 3:6], -0.5, None, ALU.mult)
                chain(dve.tensor_scalar(parts[:, :, 9:12], parts[:, :, 0:3], -0.5, None, ALU.mult))
                for i, (a, b) in enumerate(((0, 0), (0, 1), (1, 0), (1, 1), (0, 2), (2, 0))):
                    dve.tensor_copy(nu[:, :, KA + i:KA + i + 7:6], parts[:, :, a:a + 4:3])
                    dve.tensor_copy(nv[:, :, KA + i:KA + i + 7:6], parts[:, :, 6 + b:6 + b + 4:3])
                dve.memset(nu[:, :, KA + 12:KA + 15], 1.0)
                dve.memset(nu[:, :, KA + 15:KA + 16], 0.0)
                for i, part in enumerate(ROOT_PARTS):
                    dve.memset(nv[:, :, KA + 12 + i:KA + 13 + i], part / 2)
                dve.memset(nv[:, :, KA + 15:KA + 16], 0.0).then_inc(nat, 1)
                for n, (b0, (dst, _, _, k, factor)) in enumerate(turns5[1]):
                    w = min(8, NB - b0) * P
                    dve.wait_ge(ft_t, len(turns5[0]) + n + 1)
                    dve.tensor_scalar(dst[:, b0 * P:b0 * P + w], turned5(1, n, k)[:, 0:w], factor, None, ALU.mult).then_inc(ft_v, 1)
                chain(dve.scalar_tensor_tensor(g1, g1, C3, beta, ALU.mult, ALU.mult))
                chain(dve.tensor_tensor(bg1, bb, g1, ALU.mult))
                over_chunks(dve, near)
                linked[0], saved = saved, linked[0]
            with dve.Else():
                NT = (NB + 3) // 4
                chain(dve.memset(gu[:, :, D + 1:D + 3], 1.0))
                chain(dve.tensor_copy(gu[:, :, 0:D], x3))
                dve.tensor_copy(gu[:, :, D], nrm).then_inc(nat, 1)
                dve.wait_ge(ft_c, RING + NT)
                chain(dve.memset(gu[:, :, D + 2:D + 3], 0.0))
                chain(dve.memset(gu[:, :, D:D + 1], 1.0))
                dve.tensor_scalar(gu[:, :, 0:D], x3, -2.0, None, ALU.mult)
                dve.tensor_copy(gu[:, :, D + 1], nrm).then_inc(nat, 1)
                dve.wait_ge(ft_c, RING + 2 * NT)
                chain(dve.memset(gu[:, :, D + 1:D + 2], 1.0))
                dve.tensor_copy(gu[:, :, D], nrm).then_inc(nat, 1)
                dve.tensor_copy(nf[:, :, 0:D], x3)
                dve.tensor_scalar(nf[:, :, D], nrm, 1.0, None, ALU.add)
                chain(dve.tensor_tensor(bg1, bb, g1, ALU.mult))
                KG = 26

                def general(t, par, cnt, first, nxt):
                    w = cnt * P
                    with dve.Fori(0, NB) as jb:
                        it = t * NB + jb
                        n = [0]

                        def step(ins):
                            n[0] += 1
                            ins.then_inc(gc, 1)
                            dve.wait_ge(gc, it * KG + n[0])

                        dm, rec, r, root, z, lp, lm, f, qq, mask, tmp = (g[:, 0:w] for g in gen[0:11])
                        den, d2 = banks[:, 5, 0:w], banks[:, 4, 0:w]
                        dve.wait_ge(g_done, it + 1)
                        step(dve.tensor_scalar(dm, den, MIN_NORM, None, ALU.max))
                        step(dve.reciprocal(rec, dm))
                        step(dve.scalar_tensor_tensor(r, d2, 0.0, rec, ALU.max, ALU.mult))
                        step(dve.tensor_scalar(r, r, MIN_NORM * MIN_NORM, None, ALU.max))
                        dve.sem_inc(gv, 1)
                        dve.wait_ge(ga, 2 * it + 1)
                        step(dve.tensor_scalar(z, root, TANH_CLIP, None, ALU.min))
                        dve.sem_inc(gv, 1)
                        step(dve.tensor_scalar(qq, r, SMALL, None, ALU.min))
                        step(dve.tensor_scalar(mask, r, SMALL, None, ALU.is_gt))
                        step(dve.tensor_scalar(f, qq, 1 / 13, SERIES[0], ALU.mult, ALU.add))
                        for coef in SERIES[1:]:
                            step(dve.tensor_tensor(f, f, qq, ALU.mult))
                            step(dve.tensor_scalar(f, f, coef, None, ALU.add))
                        step(dve.reciprocal(tmp, root))
                        dve.wait_ge(ga, 2 * it + 2)
                        step(dve.tensor_tensor(lp, lp, lm, ALU.subtract))
                        step(dve.scalar_tensor_tensor(lp, lp, 0.5, tmp, ALU.mult, ALU.mult))
                        step(dve.tensor_tensor(lp, lp, mask, ALU.mult))
                        step(dve.tensor_scalar(mask, mask, -1.0, 1.0, ALU.mult, ALU.add))
                        step(dve.tensor_tensor(f, f, mask, ALU.mult))
                        step(dve.tensor_tensor(f, f, lp, ALU.add))
                        step(dve.tensor_tensor(f, f, rec, ALU.mult))
                        assert n[0] == KG, n[0]
                        dve.wait_ge(arrived, t + (6 * HB - 1))
                        dve.wait_ge(s_used, it + S_RING)
                        by_j = a_slot[:, par * STEP6:par * STEP6 + cnt].rearrange("p s j i -> p j s i")
                        dve.tensor_tensor(split(gen_s, cnt), split(f, cnt), by_j[:, jb, :, :], ALU.mult)\
                            .then_inc(t_rdy, 1)
                        if not first:
                            with dve.If(jb == 8):
                                dve.sem_inc(a_used, 1)
                                gather6(t - 1, STEP6)
                            with dve.Else():
                                dve.wait_ge(fl_i, 1)
                            with dve.If(jb == 20):
                                read6(t - 1, STEP6)
                            with dve.Else():
                                dve.wait_ge(fl_i, 1)

                over_chunks(dve, general)
                for _ in final_parts(0, EARLY, 0, FULL6 - 2):
                    pass
            gather6(FULL6, REST6)
            read6(FULL6, REST6)

            for _ in final_parts(EARLY, NB - EARLY, 1, FULL6 + 1):
                pass


def kernel(**inputs):
    import numpy as np
    import ml_dtypes
    import concourse.bacc as _bacc
    from concourse import mybir as _mybir
    from concourse.bass_utils import run_bass_kernel_spmd as _run

    g = {k: np.ascontiguousarray(v) for k, v in inputs.items()}
    f32 = np.float32
    adj = np.zeros((NP, NP), f32)
    adj[:N, :N] = g["adj"]
    a_blocks = np.ascontiguousarray(adj.reshape(NB, P, NB, P).transpose(0, 3, 2, 1)).reshape(NB, P, NB * P)
    xt = np.zeros((D + 1, NP), f32)
    xt[:D, :N] = g["x"].T
    xt[D] = 1.0
    w = g["L0_gnn_weights"]
    wcat = np.zeros((D + 1, 4 * D), f32)
    for i, k in enumerate((3, 2, 1, 0)):
        wcat[:D, i * D:(i + 1) * D] = w[k]
    wcat[D, 3 * D:] = g["L0_gnn_bias"]
    consts = np.zeros((P, NCONST), f32)

    def put(name, a, row=0, col=0):
        first = COLS[name][0] + col
        consts[row:row + a.shape[0], first:first + a.shape[1]] = a

    put("ident", np.eye(P, dtype=f32))
    for half in (0, D):
        put("lw3", g["L3_gnn_weight"], half, half)
    put("sel", (np.arange(P) % QUARTER == QUARTER - 1).astype(f32)[:, None])
    for half in (0, D):
        put("fold", np.eye(D, dtype=f32), half)
        put("bt", g["L1_gnn_B"].T, half)
        put("lw2", g["L2_gnn_weight"], half)
    put("qb", g["L1_gnn_B"].T)
    put("qb", np.eye(D, dtype=f32), D)
    put("w1", g["L1_gnn_W1"][:D], D)
    put("w2", g["L1_gnn_W2"])
    for name, key in (("b2", "L1_gnn_b2"), ("lb2", "L2_gnn_bias"), ("lb3", "L3_gnn_bias")):
        put(name, np.repeat(g[key][None], P, 0))
    put("tcol", np.repeat(g["L1_gnn_t"][None], P, 0))
    put("w1t", g["L1_gnn_W1"][D][:, None])
    put("b1", g["L1_gnn_b1"][:, None])
    put("valid", (np.arange(P) < N - (NB - 1) * P).astype(f32)[:, None])
    put("one", np.ones((P, 1), f32))
    k, j = np.indices((P, P))
    t0 = np.where(k > j, -UNIT, 0) + np.where(k == j, UNIT * DIAG, 0)
    t1 = -UNIT - t0
    tri = np.stack([t0, t1, np.eye(P)], 1).astype(ml_dtypes.bfloat16)

    nc = _bacc.Bacc("TRN2", target_bir_lowering=False, num_devices=1)
    arrays = {"a_blocks": a_blocks, "xt": xt, "wcat": wcat, "consts": consts, "tri": tri}
    args = [nc.dram_tensor(n, a.shape, _mybir.dt.from_np(a.dtype), kind="ExternalInput").ap() for n, a in arrays.items()]
    args.append(nc.dram_tensor("out", (N, D), _mybir.dt.float32, kind="ExternalOutput").ap())
    gnn_kernel(nc, *args)
    r = _run(nc, [arrays], core_ids=[0])
    return r.results[0]["out"]
```
